# Optimizing a Trainium2 kernel written in Bass

```python
import numpy as np
import jax
import jax.numpy as jnp

def _softmax(x, axis=-1):
    return jax.nn.softmax(x, axis=axis)

def _gelu(x):
    return jax.nn.gelu(x, approximate=True)

def _silu(x):
    return jax.nn.silu(x)

def _sigmoid(x):
    return jax.nn.sigmoid(x)

def _layernorm(x, axis=-1, eps=1e-05):
    m = jnp.mean(x, axis=axis, keepdims=True)
    v = jnp.var(x, axis=axis, keepdims=True)
    return (x - m) / jnp.sqrt(v + eps)

def _scatter_add(tgt, idx, src, axis=0):
    return tgt.at[idx].add(src)

def _segment_sum(src, seg, n):
    return jax.ops.segment_sum(src, seg, n)
kernel_name = 'mk_flamingo_gated_d2_seqx_r4_31cd4d'

def setup_inputs(seed: int=0):
    np.random.seed(seed)
    _w = jnp.asarray

    def _rec_inputs():
        import jax
        import jax.numpy as jnp
        _rk = jax.random.key(seed)
        x = 7.22e-05 + 1 * jax.random.normal(jax.random.fold_in(_rk, 1), (8, 512, 256), jnp.float32)
        _lenS = 512 - jax.random.randint(jax.random.fold_in(_rk, 7), (8,), 0, max(1, 512 // 4) + 1, jnp.int32)
        _lenS2 = 64 - jax.random.randint(jax.random.fold_in(_rk, 8), (8,), 0, max(1, 64 // 4) + 1, jnp.int32)
        _ctx_1024P = jax.random.normal(jax.random.fold_in(_rk, 11), (8, 16, 256), jnp.float32)
        _ctx_1024c = jax.random.dirichlet(jax.random.fold_in(_rk, 511), 0.3 * jnp.ones((16,), jnp.float32), (8, 64))
        _ctx_1024t = jnp.einsum('bsk,bkd->bsd', _ctx_1024c, _ctx_1024P)
        _ctx_1024t = _ctx_1024t * jax.lax.rsqrt(jnp.mean(jnp.square(_ctx_1024t)) + 1e-12) * 0.953939
        ctx_1024 = 4.13588e-05 + 0.999923 * (_ctx_1024t + 0.3 * jax.random.normal(jax.random.fold_in(_rk, 611), (8, 64, 256), jnp.float32))
        fside_BxSxS2_0 = -1.47943e-05 + 1.00017 * jax.random.normal(jax.random.fold_in(_rk, 12), (8, 512, 64), jnp.float32)
        _validS = jnp.arange(512)[None, :] < _lenS[:, None]
        _validS2 = jnp.arange(64)[None, :] < _lenS2[:, None]
        _causal = jnp.tril(jnp.ones((512, 512), dtype=bool))
        mask_BxS_ff1 = jnp.where(jnp.ones((8, 512), dtype=bool), 1.0, 0.0).astype(jnp.float32)
        mask_BxS2_ik0 = jnp.where(jnp.broadcast_to(_validS2[:, :], (8, 64)), 0, 1).astype(jnp.int32)
        _g = jax.random.normal(jax.random.fold_in(_rk, 9001), (2, 2), jnp.float32)
        _g = jnp.sign(_g) * jnp.maximum(jnp.abs(_g), 1.0) + (_g == 0) * 1.0
        g_xattn = _g[0]
        g_ffn = _g[1]
        return (x, ctx_1024, fside_BxSxS2_0, mask_BxS_ff1, mask_BxS2_ik0, g_xattn, g_ffn)
    x, ctx_1024, fside_BxSxS2_0, mask_BxS_ff1, mask_BxS2_ik0, g_xattn, g_ffn = _rec_inputs()

    def _L0_xattn_setup():
        import jax, jax.numpy as jnp
        import numpy as np
        D = 256
        key = jax.random.key(seed)
        ks = jax.random.split(key, 13)
        B, S, d = (4, 512, D)
        inp = {'q_in': jax.random.normal(ks[0], (B, S, d), jnp.float32), 'k_in': jax.random.normal(ks[1], (B, S, d), jnp.float32), 'v_in': jax.random.normal(ks[2], (B, S, d), jnp.float32), 'phi_risk': jax.random.normal(ks[3], (B, S, S), jnp.float32), 'phi_prio': jax.random.normal(ks[4], (B, S, S), jnp.float32), 'phi_impl': jax.random.normal(ks[5], (B, S, S), jnp.float32), 'Wq': jax.random.normal(ks[6], (d, d), jnp.float32) / np.sqrt(d), 'bq': jax.random.normal(ks[7], (d,), jnp.float32) * 0.01, 'Wk': jax.random.normal(ks[8], (d, d), jnp.float32) / np.sqrt(d), 'bk': jax.random.normal(ks[9], (d,), jnp.float32) * 0.01, 'Wv': jax.random.normal(ks[10], (d, d), jnp.float32) / np.sqrt(d), 'bv': jax.random.normal(ks[11], (d,), jnp.float32) * 0.01, 'beta_risk': jnp.float32(0.1), 'beta_prio': jnp.float32(0.1), 'beta_impl': jnp.float32(0.1)}
        return inp
    _L0_xattn_all = _L0_xattn_setup()
    _L0_xattn_in = {k: v for k, v in _L0_xattn_all.items() if k in ('Wq', 'bq', 'Wk', 'bk', 'Wv', 'bv', 'beta_risk', 'beta_prio', 'beta_impl')}
    del _L0_xattn_all

    def _L0_ffn_setup():
        import jax, jax.numpy as jnp
        import numpy as np
        B, S, H, I, E_ROUTED, TOP_K = (8, 512, 256, 512, 8, 2)

        def _expert(x, Wg, Wu, Wd):
            return jax.nn.silu(x @ Wg.T) * (x @ Wu.T) @ Wd.T
        key = jax.random.key(seed)
        ks = jax.random.split(key, 9)
        s = 0.02
        return {'x': jax.random.normal(ks[0], (B, S, H), dtype=jnp.float32), 'Wg_s': jax.random.normal(ks[1], (I, H), dtype=jnp.float32) * s, 'Wu_s': jax.random.normal(ks[2], (I, H), dtype=jnp.float32) * s, 'Wd_s': jax.random.normal(ks[3], (H, I), dtype=jnp.float32) * s, 'Wg': jax.random.normal(ks[4], (E_ROUTED, I, H), dtype=jnp.float32) * s, 'Wu': jax.random.normal(ks[5], (E_ROUTED, I, H), dtype=jnp.float32) * s, 'Wd': jax.random.normal(ks[6], (E_ROUTED, H, I), dtype=jnp.float32) * s, 'Wr': jax.random.normal(ks[7], (E_ROUTED, H), dtype=jnp.float32) * s, 'rb': jnp.zeros((E_ROUTED,), dtype=jnp.float32)}
    _L0_ffn_all = _L0_ffn_setup()
    _L0_ffn_in = {k: v for k, v in _L0_ffn_all.items() if k in ('Wg_s', 'Wu_s', 'Wd_s', 'Wg', 'Wu', 'Wd', 'Wr', 'rb')}
    del _L0_ffn_all

    def _L1_xattn_setup():
        import jax, jax.numpy as jnp
        import numpy as np
        B, F, T, D = (8, 64, 32, 256)
        NEG = -1e+30
        key = jax.random.key(seed)
        ks = jax.random.split(key, 10)
        s = 1.0 / np.sqrt(D)
        return {'features': jax.random.normal(ks[0], (B, F, D), jnp.float32), 'masks': jnp.ones((B, F), jnp.float32), 'textual_features': jax.random.normal(ks[1], (B, T, D), jnp.float32), 'q_masks': jax.random.randint(ks[2], (B, T), 0, 2, jnp.int32), 'Ws': jax.random.normal(ks[3], (D, D), jnp.float32) * s, 'W': jax.random.normal(ks[4], (D, D), jnp.float32) * s, 'w': jax.random.normal(ks[5], (D, 1), jnp.float32) * s, 'b': jax.random.normal(ks[6], (1, D), jnp.float32) * s, 'Wcw': jax.random.normal(ks[7], (1, D), jnp.float32) * s, 'bcw': jnp.zeros((1,), jnp.float32), 'Wcb': jax.random.normal(ks[8], (1, D), jnp.float32) * s, 'bcb': jnp.zeros((1,), jnp.float32)}
    _L1_xattn_all = _L1_xattn_setup()
    _L1_xattn_in = {k: v for k, v in _L1_xattn_all.items() if k in ('Ws', 'W', 'w', 'b', 'Wcw', 'bcw', 'Wcb', 'bcb')}
    del _L1_xattn_all

    def _L1_ffn_setup():
        import jax, jax.numpy as jnp
        import numpy as np
        B, S, D_IN, D_OUT = (16, 1024, 256, 256)
        ACT_BITS = 8
        QB = float(2 ** (ACT_BITS - 1) - 1)
        key = jax.random.key(seed)
        k1, k2, k3 = jax.random.split(key, 3)
        x = jax.random.normal(k1, (B, S, D_IN), dtype=jnp.float32)
        ternary_weight = jax.random.randint(k2, (D_OUT, D_IN), 0, 3, dtype=jnp.int32)
        bias = jax.random.normal(k3, (D_OUT,), dtype=jnp.float32)
        act_scale = (jnp.max(jnp.abs(x)) / QB).astype(jnp.float32)
        return {'x': x, 'ternary_weight': ternary_weight, 'bias': bias, 'act_scale': act_scale}
    _L1_ffn_all = _L1_ffn_setup()
    _L1_ffn_in = {k: v for k, v in _L1_ffn_all.items() if k in ('ternary_weight', 'bias', 'act_scale')}
    del _L1_ffn_all
    return {'x': x, 'ctx_1024': ctx_1024, 'fside_BxSxS2_0': fside_BxSxS2_0, 'mask_BxS_ff1': mask_BxS_ff1, 'mask_BxS2_ik0': mask_BxS2_ik0, 'g_xattn': g_xattn, 'g_ffn': g_ffn, 'L0_xattn_Wq': _L0_xattn_in['Wq'], 'L0_xattn_bq': _L0_xattn_in['bq'], 'L0_xattn_Wk': _L0_xattn_in['Wk'], 'L0_xattn_bk': _L0_xattn_in['bk'], 'L0_xattn_Wv': _L0_xattn_in['Wv'], 'L0_xattn_bv': _L0_xattn_in['bv'], 'L0_xattn_beta_risk': _L0_xattn_in['beta_risk'], 'L0_xattn_beta_prio': _L0_xattn_in['beta_prio'], 'L0_xattn_beta_impl': _L0_xattn_in['beta_impl'], 'L0_ffn_Wg_s': _L0_ffn_in['Wg_s'], 'L0_ffn_Wu_s': _L0_ffn_in['Wu_s'], 'L0_ffn_Wd_s': _L0_ffn_in['Wd_s'], 'L0_ffn_Wg': _L0_ffn_in['Wg'], 'L0_ffn_Wu': _L0_ffn_in['Wu'], 'L0_ffn_Wd': _L0_ffn_in['Wd'], 'L0_ffn_Wr': _L0_ffn_in['Wr'], 'L0_ffn_rb': _L0_ffn_in['rb'], 'L1_xattn_Ws': _L1_xattn_in['Ws'], 'L1_xattn_W': _L1_xattn_in['W'], 'L1_xattn_w': _L1_xattn_in['w'], 'L1_xattn_b': _L1_xattn_in['b'], 'L1_xattn_Wcw': _L1_xattn_in['Wcw'], 'L1_xattn_bcw': _L1_xattn_in['bcw'], 'L1_xattn_Wcb': _L1_xattn_in['Wcb'], 'L1_xattn_bcb': _L1_xattn_in['bcb'], 'L1_ffn_ternary_weight': _L1_ffn_in['ternary_weight'], 'L1_ffn_bias': _L1_ffn_in['bias'], 'L1_ffn_act_scale': _L1_ffn_in['act_scale']}

def reference(x, ctx_1024, fside_BxSxS2_0, mask_BxS_ff1, mask_BxS2_ik0, g_xattn, g_ffn, L0_xattn_Wq, L0_xattn_bq, L0_xattn_Wk, L0_xattn_bk, L0_xattn_Wv, L0_xattn_bv, L0_xattn_beta_risk, L0_xattn_beta_prio, L0_xattn_beta_impl, L0_ffn_Wg_s, L0_ffn_Wu_s, L0_ffn_Wd_s, L0_ffn_Wg, L0_ffn_Wu, L0_ffn_Wd, L0_ffn_Wr, L0_ffn_rb, L1_xattn_Ws, L1_xattn_W, L1_xattn_w, L1_xattn_b, L1_xattn_Wcw, L1_xattn_bcw, L1_xattn_Wcb, L1_xattn_bcb, L1_ffn_ternary_weight, L1_ffn_bias, L1_ffn_act_scale):
    import jax
    import jax.numpy as jnp

    def _L0_xattn_ref(q_in, k_in, v_in, phi_risk, phi_prio, phi_impl, Wq, bq, Wk, bk, Wv, bv, beta_risk, beta_prio, beta_impl):
        import jax, jax.numpy as jnp
        import numpy as np
        D = 256
        d = q_in.shape[-1]
        scale = jnp.asarray(d, q_in.dtype) ** (-0.5)
        Q = q_in @ Wq.T + bq
        K = k_in @ Wk.T + bk
        V = v_in @ Wv.T + bv
        att = jnp.einsum('bsd,btd->bst', Q, K) * scale
        att = att + beta_risk * phi_risk + beta_prio * phi_prio - beta_impl * phi_impl
        w = jax.nn.softmax(att, axis=-1)
        return jnp.einsum('bst,btd->bsd', w, V)

    def _L0_ffn_ref(x, Wg_s, Wu_s, Wd_s, Wg, Wu, Wd, Wr, rb):
        import jax, jax.numpy as jnp
        import numpy as np
        B, S, H, I, E_ROUTED, TOP_K = (8, 512, 256, 512, 8, 2)

        def _expert(x, Wg, Wu, Wd):
            return jax.nn.silu(x @ Wg.T) * (x @ Wu.T) @ Wd.T
        shared = _expert(x, Wg_s, Wu_s, Wd_s)
        logits = jnp.einsum('bsh,eh->bse', x, Wr) + rb
        probs = jax.nn.sigmoid(logits)
        scores, idx = jax.lax.top_k(probs, TOP_K)
        cw = (jax.nn.one_hot(idx, E_ROUTED, dtype=x.dtype) * scores[..., None]).sum(-2)
        out = shared
        for e in range(E_ROUTED):
            out = out + cw[..., e:e + 1] * _expert(x, Wg[e], Wu[e], Wd[e])
        return out

    def _L1_xattn_ref(features, masks, textual_features, q_masks, Ws, W, w, b, Wcw, bcw, Wcb, bcb):
        import jax, jax.numpy as jnp
        import numpy as np
        B, F, T, D = (8, 64, 32, 256)
        NEG = -1e+30
        txt_proj = jnp.einsum('btd,de->bte', textual_features, Ws)
        feat_proj = jnp.einsum('bfd,de->bfe', features, W)
        h = jnp.tanh(txt_proj[:, None, :, :] + feat_proj[:, :, None, :] + b[None, None, :, :][..., 0, :])
        rho = jnp.einsum('bftd,d->bft', h, w[:, 0])
        qm = q_masks.astype(jnp.float32)
        rho = rho + (1.0 - qm)[:, None, :] * NEG
        att = jax.nn.softmax(rho, axis=-1)
        txt_h = jnp.einsum('bft,btd->bfd', att, textual_features)
        w_s = jnp.tanh(jnp.einsum('bfd,od->bfo', txt_h, Wcw) + bcw)
        b_s = jnp.tanh(jnp.einsum('bfd,od->bfo', txt_h, Wcb) + bcb)
        return w_s * features + b_s

    def _L1_ffn_ref(x, ternary_weight, bias, act_scale):
        import jax, jax.numpy as jnp
        import numpy as np
        B, S, D_IN, D_OUT = (16, 1024, 256, 256)
        ACT_BITS = 8
        QB = float(2 ** (ACT_BITS - 1) - 1)
        scale = jnp.maximum(act_scale, 1e-05)
        x_int = jnp.clip(jnp.round(x / scale), -QB, QB)
        x_dq = jnp.nan_to_num(x_int * scale, nan=0.0, posinf=10000.0, neginf=-10000.0)
        w = ternary_weight.astype(jnp.float32) - 1.0
        return jnp.einsum('bsi,oi->bso', x_dq, w) + bias
    x = x + jnp.tanh(g_xattn[0]) * _L0_xattn_ref(_layernorm(x, axis=-1), ctx_1024, ctx_1024, fside_BxSxS2_0, fside_BxSxS2_0, fside_BxSxS2_0, L0_xattn_Wq, L0_xattn_bq, L0_xattn_Wk, L0_xattn_bk, L0_xattn_Wv, L0_xattn_bv, L0_xattn_beta_risk, L0_xattn_beta_prio, L0_xattn_beta_impl)
    x = x + jnp.tanh(g_ffn[0]) * _L0_ffn_ref(_layernorm(x, axis=-1), L0_ffn_Wg_s, L0_ffn_Wu_s, L0_ffn_Wd_s, L0_ffn_Wg, L0_ffn_Wu, L0_ffn_Wd, L0_ffn_Wr, L0_ffn_rb)
    x = x + jnp.tanh(g_xattn[1]) * _L1_xattn_ref(_layernorm(x, axis=-1), mask_BxS_ff1, ctx_1024, mask_BxS2_ik0, L1_xattn_Ws, L1_xattn_W, L1_xattn_w, L1_xattn_b, L1_xattn_Wcw, L1_xattn_bcw, L1_xattn_Wcb, L1_xattn_bcb)
    x = x + jnp.tanh(g_ffn[1]) * _L1_ffn_ref(_layernorm(x, axis=-1), L1_ffn_ternary_weight, L1_ffn_bias, L1_ffn_act_scale)
    return x

_drawn_inputs = setup_inputs


def setup_inputs(seed=0):
    import zlib

    import numpy as np

    out = dict(_drawn_inputs(seed))
    spreads = {'g_ffn': (-1.0, 0.2), 'L0_ffn_rb': (0.0, 0.7)}
    factors = {'fside_BxSxS2_0': 3.773,
     'L0_xattn_bq': 8.0,
     'L0_xattn_bk': 64.0,
     'L0_xattn_bv': 4.536,
     'L0_ffn_Wg_s': 2.756,
     'L0_ffn_Wu_s': 2.667,
     'L0_ffn_Wg': 3.221,
     'L0_ffn_Wu': 3.203,
     'L0_ffn_Wd': 3.2,
     'L0_ffn_Wr': 3.554,
     'L1_xattn_Ws': 5.735,
     'L1_xattn_W': 8.0,
     'L1_xattn_w': 3.781,
     'L1_xattn_b': 59.547}
    for name, (base, spread) in spreads.items():
        noise = np.random.default_rng([zlib.crc32(name.encode()), seed]).standard_normal(out[name].shape)
        drawn = base * np.exp(spread * noise) if base else spread * noise
        out[name] = jnp.asarray(drawn.astype(out[name].dtype))
    for name, factor in factors.items():
        out[name] = (out[name] * factor).astype(out[name].dtype)
    return out
```

```python
from contextlib import ExitStack

import concourse.bass as bass
from concourse import mybir

F32 = mybir.dt.float32
BF16 = mybir.dt.bfloat16
I32 = mybir.dt.int32
U32 = mybir.dt.uint32
ALU = mybir.AluOpType
ACT = mybir.ActivationFunctionType
AX = mybir.AxisListType.X

P = 128
LN_EPS = 1e-5
NEG = -1e30
MIN_SCALE = 1e-5
QMAX = 127.0
ROUND = 1.5 * 2 ** 23
FLT_MAX = 3.4028234e38

GROUPS = [[0, 1], [2, 3], [4, 5], [6], [7]]


class Lane:

    def __init__(self, sem):
        self.sem, self.count, self.ops, self.seen, self.last = sem, 0, [], {}, None

    def wait(self, *tokens):
        for sem, value in tokens:
            if self.seen.get(sem.name, 0) < value:
                self.seen[sem.name] = value
                self.ops.append(lambda e, s=sem, v=value: e.wait_ge(s, v))

    def do(self, instruction, *after):
        self.wait(*after)
        self.count += 1
        self.ops.append(lambda e: instruction(e).then_inc(self.sem, 1))
        self.last = (self.sem, self.count)
        return self.last

    def then(self, instruction, *after):
        return self.do(instruction, self.last, *after)

    def quiet(self, instruction):
        self.ops.append(instruction)

    def dma(self, transfer, gate, *after):
        self.wait(*after)
        gate.count += 16
        self.ops.append(lambda e: transfer(e).then_inc(gate.sem, 16))
        return (gate.sem, gate.count)


class Gate:

    def __init__(self, sem):
        self.sem, self.count = sem, 0

    def token(self):
        return (self.sem, self.count)


class Slot:

    def __init__(self, ap, gate=None):
        self.ap, self.gate, self.free, self.ready = ap, gate, [], None

    def take(self):
        assert self.free is not None, "taken before its last user gave it back"
        tokens, self.free = self.free, None
        return tokens


class Ring:
    def __init__(self, slots):
        self.slots, self.at = slots, -1

    def next(self):
        self.at += 1
        slot = self.slots[self.at % len(self.slots)]
        return slot


def merge(*lists):
    keyed = [((i + 0.5) / len(l), n, i, s) for n, l in enumerate(lists) for i, s in enumerate(l)]
    return [s for _, _, _, s in sorted(keyed, key=lambda k: k[:3])]


def build(nc, a):
    B, S, D = a["x"].shape
    T = a["fside"].shape[2]
    E, _, I = a["WgT"].shape
    DC, IC, ST = D // P, I // P, S // P
    BT = B * T
    SCALE = float(D) ** -0.5
    EW = 2 * DC * I + IC * D
    GT = [len(g) * ST for g in GROUPS]
    RT = [2 * n + E - 1 for n in GT]
    NTM, RTM = max(GT), max(RT)
    assert sum(GROUPS, []) == list(range(B)) and D == 2 * P and T == 64 and S == 512 and I == 512

    ctx = ExitStack()
    with ctx:
        def sb(name, shape, dt=F32):
            return ctx.enter_context(nc.sbuf_tensor(name, shape, dt))

        def sem(name):
            return ctx.enter_context(nc.semaphore(name))

        def gate(name):
            return Gate(sem(name))

        expert_w = sb("expert_w", [P, E, EW])
        shared_w = sb("shared_w", [P, EW])
        stream = Ring([Slot(sb(f"x{i}", [P, ST, D]), gate(f"s_x{i}")) for i in range(6)])
        normT = Slot(sb("normT", [P, DC * S]))
        featT = [Slot(sb(f"featT{c}", [P, S])) for c in range(DC)]
        normed = Ring([Slot(sb(f"normed{i}", [P, D]), gate(f"s_normed{i}")) for i in range(4)])
        wide = Ring([Slot(sb(f"wide{i}", [P, 1024])) for i in range(3)])
        attn_work, out_work = Slot(sb("attn_work", [P, 1024])), Slot(sb("out_work", [P, 1024]))
        act = Ring([Slot(sb(f"act{i}", [P, I])) for i in range(2)])
        actT = Slot(sb("actT", [P, I]))
        rows_in = Ring([Slot(sb(f"rows_in{i}", [P, D]), gate(f"s_rows_in{i}")) for i in range(2)])
        rowsT = Slot(sb("rowsT", [P, D]))
        rows_out = Ring([Slot(sb(f"rows_out{i}", [P, D]), gate(f"s_rows_out{i}")) for i in range(2)])
        picked = Ring([Slot(sb(f"picked{i}", [P, D]), gate(f"s_picked{i}")) for i in range(3)])
        score = Slot(sb("score", [P, ST, T]), gate("s_score"))
        rho = sb("rho", [P, ST, T])
        rho_e = sb("rho_e", [P, ST, T])

        txtT = sb("txtT", [P, DC, BT])
        keysq = sb("keysq", [P, DC, BT])
        values = sb("values", [P, B // 2, D])
        feat_w = sb("feat_w", [P, DC, D])
        router_w = sb("router_w", [P, DC, E])
        tern_w = sb("tern_w", [P, DC, D], BF16)
        maskadd = sb("maskadd", [P, BT])
        mulw = sb("mulw", [P, BT])
        addw = sb("addw", [P, BT])
        lin_bias = sb("lin_bias", [P, D])
        pick_w = sb("pick_w", [P, DC, 63])
        row_qb = sb("row_qb", [1, BT])
        row_bv = sb("row_bv", [1, D])
        row_rb = sb("row_rb", [1, E])
        ident = sb("ident", [P, P])
        identb = sb("identb", [P, P], BF16)
        before = sb("before", [P, P])
        ones = sb("ones", [P, P])
        rank8 = sb("rank8", [P, E])
        below = sb("below", [P, E, E])
        steps128 = sb("steps128", [P, NTM])
        tile_id = sb("tile_id", [P, RTM])
        halves = sb("halves", [P, ST])
        cols = sb("cols", [P, 6 * DC])
        scal = sb("scal", [P, 16])
        ln = {k: dict(stats=sb(f"ln_{k}_stats", [P, ST, 6]), mv=sb(f"ln_{k}_mv", [P, NTM, 2]),
                      var=sb(f"ln_{k}_var", [P, ST]), r=sb(f"ln_{k}_r", [P, NTM]),
                      t=sb(f"ln_{k}_t", [P, ST])) for k in ("att", "moe0", "moe1", "mix0", "mix1", "lin")}
        sm = {k: sb(f"sm_{k}", [P, ST]) for k in ("amax", "asum", "rmax", "rsum", "ws", "bs", "A", "B", "t")}
        prob = sb("prob", [P, NTM, E])
        prob2 = sb("prob2", [P, NTM, E])
        hot = [sb(f"hot{k}", [P, NTM, E]) for k in range(2)]
        chosen = sb("chosen", [P, NTM + 1, E])
        posn = sb("posn", [P, NTM + 1, E])
        rt = sb("rt", [P, NTM, E])
        rt2 = sb("rt2", [P, E, E])
        rs = {k: sb(f"rs_{k}", [P, n]) for k, n in
              dict(best=NTM, tiles=E, base=E, pos=NTM, cum=E, eid=RTM).items()}
        cmp_id = sb("cmp_id", [P, RTM, E])
        slot_of = [[sb(f"slot_of{g}{k}", [P, NTM], U32) for k in range(2)] for g in range(2)]
        share = [[sb(f"share{g}{k}", [P, NTM]) for k in range(2)] for g in range(2)]
        owner = [sb(f"owner{g}", [P, RTM], I32) for g in range(2)]

        banks = [Slot(ctx.enter_context(nc.psum_tensor(f"bank{i}", [P, 512], F32))) for i in range(8)]
        up_banks = Ring([(banks[0], banks[1]), (banks[2], banks[3])])
        actT_bank, row_bank, rho_bank = banks[4], banks[5], banks[6]
        misc = Ring([banks[7], banks[0], banks[1], banks[2], banks[3], banks[4], banks[5]])

        rows_dram = [nc.dram_tensor(f"rows_by_expert{g}", (RTM * P, D), F32, kind="Internal").ap() for g in range(2)]
        outs_dram = [nc.dram_tensor(f"expert_rows{g}", (RTM * P, D), F32, kind="Internal").ap() for g in range(2)]

        V, A, PE, G, SP = (Lane(sem(n)) for n in ("s_vector", "s_scalar", "s_tensor", "s_gpsimd", "s_sync"))

        tail = expert_w[:, E - 2:E, :].rearrange("p e n -> p (e n)")
        at = [0]

        def temp(n, dt=F32):
            v = tail[:, at[0]:at[0] + n]
            at[0] += n
            return v.bitcast(dt) if dt is not F32 else v

        ctxT = temp(DC * BT).rearrange("p (c n) -> p c n", c=DC)
        wk, wv, wq, ws = (temp(DC * D).rearrange("p (c n) -> p c n", c=DC) for _ in range(4))
        keysT = temp(DC * BT).rearrange("p (c n) -> p c n", c=DC)
        spread_w = temp(2 * DC * P).rearrange("p (k n) -> p k n", n=P)
        mask_i = temp(BT, I32)
        tern_i = temp(DC * D, I32).rearrange("p (c n) -> p c n", c=DC)
        assert at[0] <= 2 * EW

        def chunked(ap):
            return ap.rearrange("(c p) n -> p c n", p=P)

        g_ctx, g_small, g_late = gate("s_ctx"), gate("s_small"), gate("s_late")
        for dst, src in ((ctxT, chunked(a["ctxT"])), (wk, chunked(a["WkT"])), (wq, chunked(a["Wq"])),
                         (wv, chunked(a["WvT"])), (ws, chunked(a["Ws"]))):
            SP.dma(lambda e, d=dst, s=src: e.dma_start(d, s), g_ctx)
        ctx_in = g_ctx.token()
        BK, TB, WW, CW, CB, BQ = (k * DC for k in range(6))
        GX, GF, BR, ASC, BCW, BCB = 0, 2, 4, 7, 8, 9
        for dst, src in ((cols[:, :], a["cols"]), (row_bv[:, :], a["bv"]), (row_rb[:, :], a["rb"]),
                         (scal[:, 0:10], a["scalars"].to_broadcast([P, 10]))):
            SP.dma(lambda e, d=dst, s=src: e.dma_start(d, s), g_small)
        small_in = g_small.token()

        for m in (ident, identb):
            c = G.do(lambda e, m=m: e.memset(m[:, :], 0.0))
            G.do(lambda e, m=m: e.affine_select(out=m[:, :], in_=m[:, :], compare_op=ALU.not_equal, fill=1.0, base=0,
                                                pattern=[[-1, P]], channel_multiplier=1), c)
        ident_ok = G.last
        c = G.do(lambda e: e.memset(before[:, :], 1.0))
        G.do(lambda e: e.affine_select(out=before[:, :], in_=before[:, :], compare_op=ALU.is_gt, fill=0.0, base=0,
                                       pattern=[[1, P]], channel_multiplier=-1), c)
        G.do(lambda e: e.memset(ones[:, :], 1.0))
        ones_ok = G.last
        G.do(lambda e: e.memset(halves[:, :], -0.5))
        for ap, pattern, base in ((rank8[:, :], [[-1, E]], E), (below[:, :, :], [[1, E], [-1, E]], 0),
                                  (steps128[:, :], [[P, NTM]], 0), (tile_id[:, :], [[1, RTM]], 0)):
            G.do(lambda e, o=ap, p=pattern, b=base: e.iota(o, pattern=p, base=b, channel_multiplier=0,
                                                           allow_small_or_imprecise_dtypes=True))
        consts_ok = G.last
        V.do(lambda e: e.tensor_scalar(below[:, :, :], below[:, :, :], 0.0, None, ALU.is_gt), consts_ok)

        zeros = picked.slots[-1]
        for w in (attn_work, zeros):
            zero_ok = V.do(lambda e, w=w: e.memset(w.ap[:, :], 0.0))
        g_zero = gate("s_zero")

        def zero_rows(r):
            src = zeros.ap[:, :].unsqueeze(1).to_broadcast([P, RTM, D])
            SP.dma(lambda e: e.dma_start(r.rearrange("(n p) d -> p n d", p=P), src), g_zero, zero_ok)
            zeros.free = [g_zero.token()]

        gates_ok = A.do(lambda e: e.activation(scal[:, GX:GX + 4], scal[:, GX:GX + 4], ACT.Tanh), small_in)
        V.wait(gates_ok)
        GX0, GX1, GF0, GF1 = (scal[:, k:k + 1] for k in (GX, GX + 1, GF, GF + 1))
        V.do(lambda e: e.tensor_tensor(scal[:, BR:BR + 1], scal[:, BR:BR + 1], scal[:, BR + 1:BR + 2], ALU.add))
        V.then(lambda e: e.tensor_tensor(scal[:, BR:BR + 1], scal[:, BR:BR + 1], scal[:, BR + 2:BR + 3], ALU.subtract))
        side_w = scal[:, BR:BR + 1]
        V.do(lambda e: e.tensor_scalar(scal[:, ASC:ASC + 1], scal[:, ASC:ASC + 1], MIN_SCALE, FLT_MAX, ALU.max, ALU.min))
        V.then(lambda e: e.reciprocal(scal[:, 10:11], scal[:, ASC:ASC + 1]))
        V.do(lambda e: e.tensor_tensor(scal[:, 11:12], scal[:, ASC:ASC + 1], GF1, ALU.mult))
        inv_step, gated_step = scal[:, 10:11], scal[:, 11:12]
        c = V.do(lambda e: e.memset(pick_w[:, :, :], 0.0))
        for k in range(DC):
            V.do(lambda e, k=k: e.tensor_copy(pick_w[:, k, 31:32], cols[:, WW + k:WW + k + 1]), c)
        for k in range(2 * DC):
            V.do(lambda e, k=k: e.tensor_copy(spread_w[:, k, :], cols[:, CW + k:CW + k + 1].to_broadcast([P, P])))
        prep_ok = V.last

        def bank_for(pe=PE):
            b = misc.next()
            PE.wait(*b.take())
            return b

        def project(out, lhs, rhs, n, bias=None, row=None, parts=P):
            b = bank_for()
            for c in range(DC):
                stop = c == DC - 1 and row is None
                f = lambda e, c=c, stop=stop: e.matmul(b.ap[0:parts, 0:n], lhs(c), rhs(c), start=c == 0, stop=stop)
                done = PE.do(f) if stop else PE.quiet(f)
            if row is not None:
                done = PE.do(lambda e: e.matmul(b.ap[0:parts, 0:n], ones[0:1, 0:parts], row, start=False, stop=True))
            if bias is None:
                b.free = [A.do(lambda e: e.activation(out, b.ap[0:parts, 0:n], ACT.Copy), done)]
            else:
                b.free = [V.do(lambda e: e.tensor_scalar(out, b.ap[0:parts, 0:n], bias, None, ALU.add), done)]

        PE.wait(ctx_in, small_in, ident_ok, ones_ok, prep_ok)
        for o in range(DC):
            project(keysT[:, o, :], lambda c, o=o: wk[:, c, o * P:(o + 1) * P], lambda c: ctxT[:, c, :], BT,
                    bias=cols[:, BK + o:BK + o + 1])
        PE.wait(V.last)
        for o in range(DC):
            project(keysq[:, o, :], lambda c, o=o: wq[:, c, o * P:(o + 1) * P], lambda c: keysT[:, c, :], BT)
        project(row_qb[0:1, :], lambda c: cols[:, BQ + c:BQ + c + 1], lambda c: keysT[:, c, :], BT, parts=1)
        for j in range(B // 2):
            project(values[:, j, :], lambda c, j=j: ctxT[:, c, 2 * T * j:2 * T * (j + 1)], lambda c: wv[:, c, :], D,
                    row=row_bv[0:1, :])
        attn_ready = [A.last]

        def late_prologue():
            for dst, src in ((feat_w[:, :, :], chunked(a["W"])), (router_w[:, :, :], chunked(a["WrT"])),
                             (tern_i, chunked(a["ternT"])), (lin_bias[:, :], a["lin_bias"].to_broadcast([P, D])),
                             (mask_i, a["mask"].to_broadcast([P, BT]))):
                SP.dma(lambda e, d=dst, s=src: e.dma_start(d, s), g_late)
            late_in = g_late.token()
            for o in range(DC):
                project(txtT[:, o, :], lambda c, o=o: ws[:, c, o * P:(o + 1) * P], lambda c: ctxT[:, c, :], BT,
                        bias=cols[:, TB + o:TB + o + 1])
            project(mulw[:, :], lambda c: spread_w[:, c, :], lambda c: ctxT[:, c, :], BT)
            project(addw[:, :], lambda c: spread_w[:, DC + c, :], lambda c: ctxT[:, c, :], BT)
            V.do(lambda e: e.tensor_scalar(tern_w[:, :, :], tern_i, 1.0, None, ALU.subtract), late_in)
            V.do(lambda e: e.tensor_scalar(maskadd[:, :], mask_i, -1.0, 1.0, ALU.mult, ALU.add))
            V.then(lambda e: e.tensor_scalar(maskadd[:, :], maskadd[:, :], NEG, None, ALU.mult))
            V.do(lambda e: e.tensor_scalar(lin_bias[:, :], lin_bias[:, :], GF1, None, ALU.mult))
            PE.wait(late_in)

        g_exp = gate("s_experts")

        def load_expert(dst, WgT, WuT, WdT, *after):
            n = DC * I
            for lo, src, rows in ((0, WgT, n), (n, WuT, n), (2 * n, WdT, IC * D)):
                inner = I if src is not WdT else D
                SP.dma(lambda e, lo=lo, s=src, r=rows, i=inner: e.dma_start(
                    dst[:, lo:lo + r].rearrange("p (c n) -> p c n", n=i), chunked(s)), g_exp, *after)

        def norm_stats(k, x, first=0):
            s = ln[k]
            for i in range(ST):
                V.do(lambda e, i=i: e.bn_stats(s["stats"][:, i, :], x[:, i, :]))
            V.wait(V.last)
            for i in range(ST):
                V.do(lambda e, i=i: e.bn_aggr(s["mv"][:, first + i, :], s["stats"][:, i, :]))
            var, r, t = s["var"][:, :], s["r"][:, first:first + ST], s["t"][:, :]
            c = V.then(lambda e: e.tensor_scalar(var, s["mv"][:, first:first + ST, 1], LN_EPS, None, ALU.add))
            c = G.do(lambda e: e.tensor_tensor(r, var, halves[:, :], ALU.pow), c)
            V.do(lambda e: e.tensor_tensor(t, r, r, ALU.mult), c)
            V.then(lambda e: e.tensor_tensor(t, t, var, ALU.mult))
            V.then(lambda e: e.tensor_scalar(t, t, -0.5, 1.5, ALU.mult, ALU.add))
            return V.then(lambda e: e.tensor_tensor(r, r, t, ALU.mult))

        def normalize(k, x, i, at, stats_ok):
            s, slot = ln[k], normed.next()
            slot.ready = V.do(lambda e: e.tensor_scalar(slot.ap[:, :], x[:, i, :], s["mv"][:, at, 0:1], s["r"][:, at:at + 1],
                                                        ALU.subtract, ALU.mult), stats_ok, *slot.take())
            slot.free = []
            return slot

        def chunks(slot):
            return slot.ap[:, :].rearrange("p (c n) -> p c n", c=DC)

        def transpose_norm(k, x, first, stats_ok, box, target):
            def pair(h):
                def step():
                    slots = [normalize(k, x, i, first + i, stats_ok[0]) for i in (2 * h, 2 * h + 1)]
                    b = bank_for()
                    for n, slot in enumerate(slots):
                        PE.wait(slot.ready)
                        for c in range(DC):
                            f = lambda e, n=n, c=c, s=slot: e.transpose(b.ap[:, (n * DC + c) * P:(n * DC + c + 1) * P],
                                                                        s.ap[:, c * P:(c + 1) * P], ident[:, :])
                            done = PE.do(f) if c == DC - 1 else PE.quiet(f)
                        slot.free = [done]
                    out = chunks(target).rearrange("p c (i n) -> p i c n", n=P)[:, 2 * h:2 * h + 2, :, :]
                    b.free = [V.do(lambda e: e.tensor_copy(out, b.ap[:, :].rearrange("p (i c n) -> p i c n", i=2, c=DC)),
                                   done, *(target.take() if h == 0 else []))]
                    box[:] = [V.last]
                return step
            return [pair(0), pair(1)]

        xs = {}
        moe_ok = {}

        def attend(b):
            st = {}
            gi = next(i for i, g in enumerate(GROUPS) if b in g)
            first = GROUPS[gi].index(b) * ST
            key = f"moe{gi % 2}"
            half = (b % 2) * T
            stats1, stats2, lnT1, lnT2 = [None], [None], [], []

            def load():
                x = xs[b] = stream.next()
                x.ready = SP.dma(lambda e: e.dma_start(x.ap[:, :, :], a["x"][b].rearrange("(i p) d -> p i d", p=P)),
                                 x.gate, *x.take())
                st["side"] = SP.dma(lambda e: e.dma_start(score.ap[:, :, :], a["fside"][b].rearrange("(i p) d -> p i d", p=P)),
                                    score.gate, *score.take())

            def stats():
                V.wait(xs[b].ready)
                stats1[0] = norm_stats("att", xs[b].ap)
                V.do(lambda e: e.tensor_scalar(score.ap[:, :, :], score.ap[:, :, :], side_w, None, ALU.mult), st["side"])

            def scores():
                bk = bank_for()
                PE.wait(*lnT1, *attn_ready)
                for i in range(ST):
                    o = bk.ap[:, i * T:(i + 1) * T]
                    PE.quiet(lambda e, o=o: e.matmul(o, ones[0:1, :], row_qb[0:1, b * T:(b + 1) * T], start=True, stop=False))
                    for c in range(DC):
                        f = lambda e, o=o, c=c, i=i: e.matmul(o, normT.ap[:, c * S + i * P:c * S + (i + 1) * P],
                                                              keysq[:, c, b * T:(b + 1) * T], start=False, stop=c == DC - 1)
                        done = PE.do(f) if c == DC - 1 and i == ST - 1 else PE.quiet(f)
                normT.free = [done]
                sc, m = score.ap, sm["amax"]
                bk.free = [V.do(lambda e: e.scalar_tensor_tensor(out=sc[:, :, :], in0=bk.ap[:, 0:ST * T].rearrange("p (i t) -> p i t", t=T),
                                                                 scalar=SCALE, in1=sc[:, :, :], op0=ALU.mult, op1=ALU.add), V.last, done)]
                V.then(lambda e: e.tensor_reduce(m[:, :], sc[:, :, :], AX, ALU.max))
                V.then(lambda e: e.tensor_tensor(sc[:, :, :], sc[:, :, :], m[:, :].unsqueeze(2).to_broadcast([P, ST, T]), ALU.subtract))
                w = st["w"] = attn_work
                ex = w.ap[:, 0:ST * P].rearrange("p (i t) -> p i t", t=P)[:, :, half:half + T]
                st["e"] = A.do(lambda e: e.activation(ex, sc[:, :, :], ACT.Exp), V.last, *w.take())
                score.free = [st["e"]]
                V.do(lambda e: e.tensor_reduce(sm["asum"][:, :], ex, AX, ALU.add), st["e"])
                V.then(lambda e: e.reciprocal(sm["asum"][:, :], sm["asum"][:, :]))
                st["sum"] = V.then(lambda e: e.tensor_scalar(sm["asum"][:, :], sm["asum"][:, :], GX0, None, ALU.mult))

            def turn():
                bk, w = bank_for(), st["w"]
                PE.wait(st["e"])
                for i in range(ST):
                    f = lambda e, i=i: e.transpose(bk.ap[:, i * P:(i + 1) * P], w.ap[:, i * P:(i + 1) * P], ident[:, :])
                    done = PE.do(f) if i == ST - 1 else PE.quiet(f)
                st["eT"] = A.do(lambda e: e.activation(w.ap[:, 512:1024], bk.ap[:, :], ACT.Copy), done)
                bk.free = [st["eT"]]

            def weigh(h):
                def step():
                    bk, w, x = bank_for(), st["w"], xs[b].ap
                    PE.wait(st["eT"])
                    for n in range(2):
                        i = 2 * h + n
                        f = lambda e, i=i, n=n: e.matmul(bk.ap[:, n * D:(n + 1) * D], w.ap[half:half + T, 512 + i * P:512 + (i + 1) * P],
                                                         values[half:half + T, b // 2, :], start=True, stop=True)
                        done = PE.do(f) if n else PE.quiet(f)
                    if h == 1:
                        w.free = [done]
                    for n in range(2):
                        i = 2 * h + n
                        V.do(lambda e, i=i, n=n: e.scalar_tensor_tensor(
                            out=x[:, i, :], in0=bk.ap[:, n * D:(n + 1) * D], scalar=sm["asum"][:, i:i + 1], in1=x[:, i, :],
                            op0=ALU.mult, op1=ALU.add), done, st["sum"])
                    bk.free = [V.last]
                return step

            def stats_moe():
                V.wait(V.last)
                stats2[0] = moe_ok[b] = norm_stats(key, xs[b].ap, first)

            def logits():
                bk = bank_for()
                PE.wait(*lnT2)
                for i in range(ST):
                    o = bk.ap[:, i * E:(i + 1) * E]
                    PE.quiet(lambda e, o=o: e.matmul(o, ones[0:1, :], row_rb[0:1, :], start=True, stop=False))
                    for c in range(DC):
                        f = lambda e, o=o, c=c, i=i: e.matmul(o, normT.ap[:, c * S + i * P:c * S + (i + 1) * P], router_w[:, c, :],
                                                              start=False, stop=c == DC - 1)
                        done = PE.do(f) if c == DC - 1 and i == ST - 1 else PE.quiet(f)
                normT.free = [done]
                pr = prob[:, first:first + ST, :]
                bk.free = [A.do(lambda e: e.activation(pr, bk.ap[:, 0:ST * E].rearrange("p (i n) -> p i n", n=E), ACT.Exp, scale=-1.0),
                                done, *prob_free)]
                V.do(lambda e: e.tensor_scalar(pr, pr, 1.0, None, ALU.add), A.last)
                V.then(lambda e: e.reciprocal(pr, pr))

            return ([load, stats] + transpose_norm("att", _Later(xs, b), 0, stats1, lnT1, normT)
                    + [scores, turn, weigh(0), weigh(1), stats_moe]
                    + transpose_norm(key, _Later(xs, b), first, stats2, lnT2, normT) + [logits])

        prob_free = []

        def route(gi):
            par, n, R, group = gi % 2, GT[gi], RT[gi], GROUPS[gi]
            pr, p2, ch, rb = prob[:, 0:n, :], prob2[:, 0:n, :], chosen[:, 0:n, :], rt[:, 0:n, :]
            best = rs["best"][:, 0:n]

            def wide_(v):
                return v.unsqueeze(2).to_broadcast([P, n, E])

            def choose():
                rank = rank8[:, :].unsqueeze(1).to_broadcast([P, n, E])
                for k in range(2):
                    src, top, h = (pr, p2)[k], share[par][k][:, 0:n], hot[k][:, 0:n, :]
                    V.then(lambda e, s=src, t=top: e.tensor_reduce(t, s, AX, ALU.max))
                    V.then(lambda e, s=src, t=top: e.tensor_tensor(rb, s, wide_(t), ALU.is_equal))
                    V.then(lambda e: e.tensor_tensor(rb, rb, rank, ALU.mult))
                    V.then(lambda e: e.tensor_reduce(best, rb, AX, ALU.max))
                    V.then(lambda e, h=h: e.tensor_tensor(h, rank, wide_(best), ALU.is_equal))
                    if k == 0:
                        V.then(lambda e, h=h: e.scalar_tensor_tensor(out=p2, in0=h, scalar=-2.0, in1=pr, op0=ALU.mult, op1=ALU.add))
                prob_free[:] = [V.last]
                V.then(lambda e: e.tensor_tensor(ch, hot[0][:, 0:n, :], hot[1][:, 0:n, :], ALU.add))
                V.do(lambda e: e.memset(chosen[:, n, :], 0.0))
                for k in range(2):
                    V.do(lambda e, k=k: e.tensor_scalar(share[par][k][:, 0:n], share[par][k][:, 0:n], GF0, None, ALU.mult))

            def count():
                bk = bank_for()
                PE.wait(V.last, consts_ok)
                W = (n + 1) * E
                PE.quiet(lambda e: e.matmul(bk.ap[:, 0:W], before[:, :], chosen[:, 0:n + 1, :].rearrange("p i e -> p (i e)"), start=True, stop=False))
                for i in range(n):
                    m = n - i
                    f = lambda e, i=i, m=m: e.matmul(bk.ap[:, (i + 1) * E:W].rearrange("p (j e) -> p j e", e=E), ones[:, :],
                                                     chosen[:, i:i + 1, :].to_broadcast([P, m, E]), start=False, stop=i == n - 1)
                    done = PE.do(f) if i == n - 1 else PE.quiet(f)
                bk.free = [V.do(lambda e: e.tensor_copy(posn[:, 0:n + 1, :].rearrange("p i e -> p (i e)"), bk.ap[:, 0:W]), done)]

            def place():
                total = posn[:, n, :]
                t2 = rt2[:, :, :]
                tiles, base, cum = (rs[k][:, :] for k in ("tiles", "base", "cum"))
                V.then(lambda e: e.tensor_tensor(rt[:, 0:n, :].rearrange("p j e -> p e j"), total.unsqueeze(2).to_broadcast([P, E, n]),
                                                 steps128[:, 0:n].unsqueeze(1).to_broadcast([P, E, n]), ALU.is_gt))
                V.then(lambda e: e.tensor_reduce(tiles, rt[:, 0:n, :].rearrange("p j e -> p e j"), AX, ALU.add))
                V.then(lambda e: e.tensor_tensor(t2, below[:, :, :], tiles.unsqueeze(1).to_broadcast([P, E, E]), ALU.mult))
                V.then(lambda e: e.tensor_reduce(base, t2, AX, ALU.add))
                V.then(lambda e: e.tensor_tensor(cum, base, tiles, ALU.add))
                V.then(lambda e: e.tensor_scalar(base, base, float(P), None, ALU.mult))
                pos = posn[:, 0:n, :]
                V.then(lambda e: e.tensor_tensor(pos, pos, base.unsqueeze(1).to_broadcast([P, n, E]), ALU.add))
                for k in range(2):
                    V.then(lambda e, k=k: e.tensor_tensor(rb, hot[k][:, 0:n, :], pos, ALU.mult))
                    V.then(lambda e: e.tensor_reduce(rs["pos"][:, 0:n], rb, AX, ALU.add))
                    V.then(lambda e, k=k: e.tensor_copy(slot_of[par][k][:, 0:n], rs["pos"][:, 0:n]), *gathers_done[par])
                cm = cmp_id[:, 0:R, :]
                V.then(lambda e: e.tensor_tensor(cm, cum.unsqueeze(1).to_broadcast([P, R, E]),
                                                 tile_id[:, 0:R].unsqueeze(2).to_broadcast([P, R, E]), ALU.is_le))
                V.then(lambda e: e.tensor_reduce(rs["eid"][:, 0:R], cm, AX, ALU.add))
                placed[gi] = V.then(lambda e: e.tensor_scalar(owner[par][:, 0:R], rs["eid"][:, 0:R], float(E - 1), None, ALU.min),
                                    *owner_free[par])

            def scatter(i):
                def step():
                    b, key = group[i // ST], f"moe{par}"
                    slot = normalize(key, xs[b].ap, i % ST, i, moe_ok[b])
                    for k in range(2):
                        tok = G.dma(lambda e, k=k: e.indirect_dma_start(
                            out=rows_dram[par], out_offset=bass.IndirectOffsetOnAxis(ap=slot_of[par][k][:, i:i + 1], axis=0),
                            in_=slot.ap[:, :], in_offset=None), slot.gate, slot.ready, placed[gi], *rows_free[par],
                            g_zero.token())
                    slot.free = [tok]
                    scattered.setdefault(gi, {})[slot.gate.sem.name] = tok
                return step

            return [choose, count, place] + [scatter(i) for i in range(n)]

        placed, scattered = {}, {}
        gathers_done = [[], []]
        owner_free = [[], []]
        rows_free = [[], []]

        tiles = [(gi, "shared", i) for gi in range(len(GROUPS)) for i in range(GT[gi])]
        tiles = []
        for gi in range(len(GROUPS)):
            tiles += [(gi, "shared", i) for i in range(GT[gi])] + [(gi, "routed", s) for s in range(RT[gi])]
        work = {}
        stored = {}

        def fetch(n):
            if n >= len(tiles) or tiles[n][1] != "routed":
                return
            gi, _, s = tiles[n]
            r = work.setdefault(n, {})["rows"] = rows_in.next()
            r.ready = SP.dma(lambda e: e.dma_start(r.ap[:, :], rows_dram[gi % 2][s * P:(s + 1) * P, :]), r.gate,
                             *r.take(), *scattered[gi].values())

        def turn_rows(n):
            if n >= len(tiles):
                return
            gi, kind, s = tiles[n]
            w = work.setdefault(n, {})
            if kind == "routed":
                r = w["rows"]
                w["owner_ok"] = placed[gi]
            else:
                b = GROUPS[gi][s // ST]
                r = normalize(f"moe{gi % 2}", xs[b].ap, s % ST, s, moe_ok[b])
            PE.wait(r.ready, *row_bank.take())
            for c in range(DC):
                f = lambda e, c=c: e.transpose(row_bank.ap[:, c * P:(c + 1) * P], r.ap[:, c * P:(c + 1) * P], ident[:, :])
                done = PE.do(f) if c == DC - 1 else PE.quiet(f)
            r.free = [done]
            if kind == "routed":
                rows_free[gi % 2] = [done]
            w["rowsT"] = V.do(lambda e: e.tensor_copy(rowsT.ap[:, :], row_bank.ap[:, 0:D]), done, *rowsT.take())
            row_bank.free = [w["rowsT"]]

        N1 = DC * I

        def widen(n):
            gi, kind, s = tiles[n]
            w = work[n]
            bg, bu = up_banks.next()
            PE.wait(w["rowsT"], experts_in[0])
            if kind == "routed":
                PE.wait(w["owner_ok"])

                def load_owner(e):
                    w["e"] = e.value_load(owner[gi % 2][0:1, s:s + 1], min_val=0, max_val=E - 1)
                PE.quiet(load_owner)
            weights = expert_w[:, :, :].rearrange("p e n -> p (e n)")

            def rhs(lo, m):
                return shared_w[:, lo:lo + m] if kind == "shared" else weights[:, bass.ds(w["e"] * EW + lo, m)]
            w["rhs"] = rhs
            toks = []
            for bank, lo in ((bg, 0), (bu, N1)):
                PE.wait(*bank.take())
                for c in range(DC):
                    f = lambda e, c=c, bank=bank, lo=lo: e.matmul(bank.ap[:, :], rowsT.ap[:, c * P:(c + 1) * P],
                                                                  rhs(lo + c * I, I), start=c == 0, stop=c == DC - 1)
                    done = PE.do(f) if c == DC - 1 else PE.quiet(f)
                toks.append(done)
            rowsT.free = [done]
            h = w["act"] = act.next()
            t = A.do(lambda e: e.activation(h.ap[:, :], bg.ap[:, :], ACT.Tanh, scale=0.5), toks[0], *h.take())
            V.do(lambda e: e.scalar_tensor_tensor(out=h.ap[:, :], in0=h.ap[:, :], scalar=1.0, in1=bg.ap[:, :],
                                                  op0=ALU.add, op1=ALU.mult), t)
            w["h"] = V.then(lambda e: e.scalar_tensor_tensor(out=h.ap[:, :], in0=h.ap[:, :], scalar=0.5, in1=bu.ap[:, :],
                                                             op0=ALU.mult, op1=ALU.mult), toks[1])
            bg.free = bu.free = [w["h"]]

        def turn_act(n):
            w = work[n]
            h = w["act"]
            PE.wait(w["h"], *actT_bank.take())
            for c in range(IC):
                f = lambda e, c=c: e.transpose(actT_bank.ap[:, c * P:(c + 1) * P], h.ap[:, c * P:(c + 1) * P], ident[:, :])
                done = PE.do(f) if c == IC - 1 else PE.quiet(f)
            h.free = [done]
            w["actT"] = A.do(lambda e: e.activation(actT.ap[:, :], actT_bank.ap[:, :], ACT.Copy), done, *actT.take())
            actT_bank.free = [w["actT"]]

        def narrow(n):
            gi, kind, s = tiles[n]
            w = work.pop(n)
            PE.wait(w["actT"], *row_bank.take())
            for c in range(IC):
                f = lambda e, c=c: e.matmul(row_bank.ap[:, 0:D], actT.ap[:, c * P:(c + 1) * P],
                                            w["rhs"](2 * N1 + c * D, D), start=c == 0, stop=c == IC - 1)
                done = PE.do(f) if c == IC - 1 else PE.quiet(f)
            actT.free = [done]
            if kind == "shared":
                x = xs[GROUPS[gi][s // ST]].ap[:, s % ST, :]
                row_bank.free = [V.do(lambda e: e.scalar_tensor_tensor(out=x, in0=row_bank.ap[:, 0:D], scalar=GF0, in1=x,
                                                                       op0=ALU.mult, op1=ALU.add), done)]
            else:
                y = rows_out.next()
                row_bank.free = [V.do(lambda e: e.tensor_copy(y.ap[:, :], row_bank.ap[:, 0:D]), done, *y.take())]
                tok = SP.dma(lambda e: e.dma_start(outs_dram[gi % 2][s * P:(s + 1) * P, :], y.ap[:, :]), y.gate,
                             row_bank.free[0], *gathers_done[gi % 2])
                y.free = [tok]
                stored.setdefault(gi, {})[y.gate.sem.name] = tok
                if s == RT[gi] - 1:
                    owner_free[gi % 2] = [done]

        def expert_steps(gi):
            lo = sum(GT[:gi]) + sum(RT[:gi])
            hi = lo + GT[gi] + RT[gi]
            last = hi == len(tiles)
            steps = []
            for n in range(lo, hi + last):
                def first(n=n):
                    if n == lo and n not in work:
                        turn_rows(n)
                    if n < len(tiles):
                        widen(n)
                    if n - 1 in work:
                        turn_act(n - 1)
                    if n + 1 < hi and n + 1 < len(tiles):
                        turn_rows(n + 1)
                    if n + 3 < hi or n == lo:
                        for m in ([n + 3] if n > lo else [n + 1, n + 2, n + 3]):
                            if m < hi:
                                fetch(m)

                def second(n=n):
                    if n - 1 in work:
                        narrow(n - 1)
                steps += [first, second]
            return steps

        def mix_in(b):
            gi = next(i for i, g in enumerate(GROUPS) if b in g)
            first, par = GROUPS[gi].index(b) * ST, gi % 2
            stats, lnT = [None], mixT[b]

            def gather(i):
                def step():
                    x = xs[b].ap[:, i, :]
                    for k in range(2):
                        y = picked.next()
                        y.ready = G.dma(lambda e, k=k, y=y: e.indirect_dma_start(
                            out=y.ap[:, :], out_offset=None, in_=outs_dram[par],
                            in_offset=bass.IndirectOffsetOnAxis(ap=slot_of[par][k][:, first + i:first + i + 1], axis=0)),
                            y.gate, *stored[gi].values(), *y.take())
                        V.wait(V.last)
                        y.free = [V.do(lambda e, k=k, y=y: e.scalar_tensor_tensor(
                            out=x, in0=y.ap[:, :], scalar=share[par][k][:, first + i:first + i + 1], in1=x,
                            op0=ALU.mult, op1=ALU.add), y.ready)]
                    gathers_done[par] = [V.last]
                return step

            def stat():
                V.wait(V.last)
                stats[0] = norm_stats(f"mix{b % 2}", xs[b].ap)
            return [gather(i) for i in range(ST)] + [stat] + transpose_norm(f"mix{b % 2}", _Later(xs, b), 0, stats, lnT, out_work)

        mixT = {b: [] for b in range(B)}
        feat_ok = {}

        def feature(b, ec):
            def step():
                bk = bank_for()
                PE.wait(*mixT[b])
                for c in range(DC):
                    f = lambda e, c=c: e.matmul(bk.ap[:, :], feat_w[:, c, ec * P:(ec + 1) * P], out_work.ap[:, c * S:(c + 1) * S],
                                                start=c == 0, stop=c == DC - 1)
                    done = PE.do(f) if c == DC - 1 else PE.quiet(f)
                if ec == DC - 1:
                    out_work.free = [done]
                feat_ok[b, ec] = V.do(lambda e: e.tensor_copy(featT[ec].ap[:, :], bk.ap[:, :]), done)
                bk.free = [feat_ok[b, ec]]
            return step

        LAG = 2
        JN = 4
        TM = T // JN
        pending = []

        def sum_unit(u):
            b, ec, m, jj, w, ready = u
            PE.wait(ready)
            if (ec, m, jj) == (0, 0, 0):
                PE.wait(*rho_bank.take())
            for n in range(2):
                j = 2 * jj + n
                f = lambda e, n=n, j=j: e.matmul(rho_bank.ap[32 * j:32 * j + 32, :], pick_w[:, ec, 31 - m:63 - m],
                                                 w.ap[:, n * S:(n + 1) * S], start=(ec, m) == (0, 0), stop=(ec, m) == (DC - 1, TM - 1))
                done = PE.do(f) if n else PE.quiet(f)
            w.free = [done]
            rho_done[b] = done

        rho_done = {}

        def tanh_steps(b, ec):
            def unit(m, jj):
                def step():
                    w = wide.next()
                    free = w.take()
                    for n in range(2):
                        t = b * T + TM * (2 * jj + n) + m
                        V.do(lambda e, n=n, t=t: e.tensor_scalar(w.ap[:, n * S:(n + 1) * S], featT[ec].ap[:, :], txtT[:, ec, t:t + 1],
                                                                 None, ALU.add), feat_ok[b, ec], *free)
                    ready = A.do(lambda e: e.activation(w.ap[:, :], w.ap[:, :], ACT.Tanh), V.last)
                    pending.append((b, ec, m, jj, w, ready))
                    if len(pending) > LAG:
                        sum_unit(pending.pop(0))
                return step
            steps = [unit(m, jj) for m in range(TM) for jj in range(2)]
            if ec == DC - 1:
                def flush():
                    while pending:
                        sum_unit(pending.pop(0))
                steps.append(flush)
            return steps

        def mix_out(b):
            st = {}
            stats4, x = [None], _Later(xs, b)

            def scores():
                w = st["w"] = out_work
                st["ev"] = V.do(lambda e: e.tensor_copy(w.ap[:, 0:S], rho_bank.ap[:, :]), rho_done[b], *w.take())
                rho_bank.free = [st["ev"]]

            def turn():
                w, bk = st["w"], bank_for()
                PE.wait(st["ev"])
                for i in range(ST):
                    f = lambda e, i=i: e.transpose(bk.ap[:, i * P:(i + 1) * P], w.ap[:, i * P:(i + 1) * P], ident[:, :])
                    done = PE.do(f) if i == ST - 1 else PE.quiet(f)
                w.free = [done]
                for i in range(ST):
                    V.do(lambda e, i=i: e.tensor_tensor(
                        rho[:, i, :].rearrange("p (j m) -> p j m", j=JN),
                        bk.ap[:, i * P:(i + 1) * P].rearrange("p (j m) -> p j m", j=JN)[:, :, 0:TM],
                        maskadd[:, b * T:(b + 1) * T].rearrange("p (j m) -> p j m", j=JN), ALU.add), done)
                bk.free = [V.last]
                V.then(lambda e: e.tensor_reduce(sm["rmax"][:, :], rho[:, :, :], AX, ALU.max))
                V.then(lambda e: e.tensor_tensor(rho[:, :, :], rho[:, :, :], sm["rmax"][:, :].unsqueeze(2).to_broadcast([P, ST, T]),
                                                 ALU.subtract))
                st["e"] = A.do(lambda e: e.activation(rho_e[:, :, :], rho[:, :, :], ACT.Exp), V.last)

            def weigh():
                V.do(lambda e: e.tensor_reduce(sm["rsum"][:, :], rho_e[:, :, :], AX, ALU.add), st["e"])
                V.then(lambda e: e.reciprocal(sm["rsum"][:, :], sm["rsum"][:, :]))
                for out, vec in (("ws", mulw), ("bs", addw)):
                    cv = vec[:, b * T:(b + 1) * T].unsqueeze(1).to_broadcast([P, ST, T])
                    V.then(lambda e, cv=cv: e.tensor_tensor(rho[:, :, :], rho_e[:, :, :], cv, ALU.mult))
                    V.then(lambda e, o=out: e.tensor_reduce(sm[o][:, :], rho[:, :, :], AX, ALU.add))
                    V.then(lambda e, o=out: e.tensor_tensor(sm[o][:, :], sm[o][:, :], sm["rsum"][:, :], ALU.mult))
                A.do(lambda e: e.activation(sm["ws"][:, :], sm["ws"][:, :], ACT.Tanh, bias=scal[:, BCW:BCW + 1]), V.last)
                st["wb"] = A.do(lambda e: e.activation(sm["bs"][:, :], sm["bs"][:, :], ACT.Tanh, bias=scal[:, BCB:BCB + 1]))

            def apply():
                own = ln[f"mix{b % 2}"]
                r, mean, Ac, Bc = own["r"][:, 0:ST], own["mv"][:, 0:ST, 0], sm["A"][:, :], sm["B"][:, :]
                V.do(lambda e: e.tensor_tensor(Ac, sm["ws"][:, :], r, ALU.mult), st["wb"])
                V.then(lambda e: e.tensor_scalar(Ac, Ac, GX1, None, ALU.mult))
                V.then(lambda e: e.tensor_tensor(sm["t"][:, :], Ac, mean, ALU.mult))
                V.then(lambda e: e.scalar_tensor_tensor(out=Bc, in0=sm["bs"][:, :], scalar=GX1, in1=sm["t"][:, :],
                                                        op0=ALU.mult, op1=ALU.subtract))
                V.then(lambda e: e.tensor_scalar(Ac, Ac, 1.0, None, ALU.add))
                V.wait(V.last)
                for i in range(ST):
                    V.do(lambda e, i=i: e.tensor_scalar(x.ap[:, i, :], x.ap[:, i, :], sm["A"][:, i:i + 1], sm["B"][:, i:i + 1],
                                                        ALU.mult, ALU.add))
                V.wait(V.last)
                stats4[0] = norm_stats("lin", x.ap)

            def quantize(i):
                def step():
                    s, o = normalize("lin", x.ap, i, i, stats4[0]), normed.next()
                    q = out_work.ap[:, S:2 * S].bitcast(BF16)[:, i * D:(i + 1) * D]
                    V.then(lambda e: e.tensor_scalar(o.ap[:, :], s.ap[:, :], inv_step, 0.0, ALU.mult, ALU.max), *o.take())
                    V.do(lambda e: e.tensor_scalar(s.ap[:, :], s.ap[:, :], inv_step, 0.0, ALU.mult, ALU.min))
                    V.then(lambda e: e.tensor_tensor(s.ap[:, :], s.ap[:, :], o.ap[:, :], ALU.add))
                    V.then(lambda e: e.tensor_scalar(s.ap[:, :], s.ap[:, :], QMAX, -QMAX, ALU.min, ALU.max))
                    V.then(lambda e: e.tensor_scalar(q, s.ap[:, :], ROUND, ROUND, ALU.add, ALU.subtract), *(out_work.take() if i == 0 else []))
                    s.free, o.free = [], []
                return step

            def turn_quant():
                w, bk = out_work, bank_for()
                pb, q = bk.ap[:, :].bitcast(BF16), w.ap[:, S:2 * S].bitcast(BF16)
                PE.wait(V.last)
                for n in range(ST * DC):
                    f = lambda e, n=n: e.transpose(pb[:, n * P:(n + 1) * P], q[:, n * P:(n + 1) * P], identb[:, :])
                    done = PE.do(f) if n == ST * DC - 1 else PE.quiet(f)
                st["qT"] = V.do(lambda e: e.tensor_copy(w.ap[:, 0:S].bitcast(BF16), pb), done)
                bk.free = [st["qT"]]

            def linear(h):
                def step():
                    w, bk = out_work, bank_for()
                    qT = w.ap[:, 0:S].bitcast(BF16)
                    PE.wait(st["qT"])
                    for n in range(2):
                        i = 2 * h + n
                        for c in range(DC):
                            f = lambda e, i=i, n=n, c=c: e.matmul(bk.ap[:, n * D:(n + 1) * D], qT[:, (i * DC + c) * P:(i * DC + c + 1) * P],
                                                                  tern_w[:, c, :], start=c == 0, stop=c == DC - 1)
                            done = PE.do(f) if n and c == DC - 1 else PE.quiet(f)
                    if h == 1:
                        w.free = [done]
                    for n in range(2):
                        xi = x.ap[:, 2 * h + n, :]
                        V.do(lambda e, xi=xi: e.tensor_tensor(xi, xi, lin_bias[:, :], ALU.add))
                        V.then(lambda e, xi=xi, n=n: e.scalar_tensor_tensor(out=xi, in0=bk.ap[:, n * D:(n + 1) * D], scalar=gated_step,
                                                                            in1=xi, op0=ALU.mult, op1=ALU.add), done)
                    bk.free = [V.last]
                    if h == 1:
                        slot = xs[b]
                        slot.free = [SP.dma(lambda e: e.dma_start(a["out"][b].rearrange("(i p) d -> p i d", p=P), slot.ap[:, :, :]),
                                            slot.gate, V.last)]
                return step

            return [scores, turn, weigh, apply] + [quantize(i) for i in range(ST)] + [turn_quant, linear(0), linear(1)]

        def mix(gi):
            g = GROUPS[gi]
            steps = mix_in(g[0]) + [feature(g[0], 0), feature(g[0], 1)]
            for n, b in enumerate(g):
                nxt = g[n + 1] if n + 1 < len(g) else None
                a0 = tanh_steps(b, 0)
                if n:
                    out = mix_out(g[n - 1])
                    a0 = merge(a0, out)
                a1 = tanh_steps(b, 1)
                flush = a1.pop()
                if nxt is not None:
                    a1 = merge(a1, mix_in(nxt) + [feature(nxt, 0)])
                steps += a0 + a1 + [flush]
                if nxt is not None:
                    steps += [feature(nxt, 1), mix_first(b)]
            return steps + mix_out(g[-1])

        outs = {}
        make_out = mix_out

        def mix_out(b):
            if b not in outs:
                outs[b] = make_out(b)
                return outs[b]
            return outs[b][1:]

        def mix_first(b):
            return mix_out_steps(b)[0]

        def mix_out_steps(b):
            if b not in outs:
                outs[b] = make_out(b)
            return outs[b]

        late_prologue()
        temps_read = [PE.last, V.last]
        experts_in = [None]

        def load_weights():
            load_expert(shared_w[:, :], a["WgsT"], a["WusT"], a["WdsT"])
            zero_rows(rows_dram[0])
            for k in range(E):
                load_expert(expert_w[:, k, :], a["WgT"][k], a["WuT"][k], a["WdT"][k], *(temps_read if k >= E - 2 else []))
            zero_rows(rows_dram[1])
            experts_in[0] = g_exp.token()

        def run(steps):
            for s in steps:
                s()

        def attends(gi):
            return [s for b in GROUPS[gi] for s in attend(b)] + route(gi)

        NG = len(GROUPS)
        first = attends(0)
        run(first[:1])
        load_weights()
        run(first[1:])
        misc.slots, misc.at = [banks[7]], 0
        for gi in range(NG):
            tile_steps = expert_steps(gi)
            run(tile_steps[:2])
            beside = [tile_steps[2:]]
            if gi + 1 < NG:
                beside.append(attends(gi + 1))
            if gi:
                beside.append(mix(gi - 1))
            run(merge(*beside))
        misc.slots = [banks[i] for i in (7, 0, 1, 2, 3, 4, 5)]
        run(mix(NG - 1))
        SP.wait(*[t for x in stream.slots for t in x.free])

        block = ctx.enter_context(nc.Block())
        for name, lane in (("sync", SP), ("gpsimd", G), ("scalar", A), ("vector", V), ("tensor", PE)):
            def body(e, lane=lane):
                for op in lane.ops:
                    op(e)
            {"sync": block.sync, "gpsimd": block.gpsimd, "scalar": block.scalar, "vector": block.vector,
             "tensor": block.tensor}[name](body)


class _Later:

    def __init__(self, xs, b):
        self.xs, self.b = xs, b

    @property
    def ap(self):
        return self.xs[self.b].ap

    def __getitem__(self, key):
        return self.xs[self.b].ap[key]


def kernel(**inputs):
    import numpy as np
    import concourse.bacc as bacc
    from concourse.bass_utils import run_bass_kernel_spmd

    i = {k: np.asarray(v) for k, v in inputs.items()}
    B, T = i["ctx_1024"].shape[0], i["ctx_1024"].shape[1]
    D = i["x"].shape[2]
    vectors = ("L0_xattn_bk", "L1_xattn_b", "L1_xattn_w", "L1_xattn_Wcw", "L1_xattn_Wcb", "L0_xattn_bq")
    cols = np.concatenate([i[n].reshape(D // P, P).T for n in vectors], axis=1)
    numbers = ("g_xattn", "g_ffn", "L0_xattn_beta_risk", "L0_xattn_beta_prio", "L0_xattn_beta_impl",
               "L1_ffn_act_scale", "L1_xattn_bcw", "L1_xattn_bcb")
    scalars = np.concatenate([i[n].reshape(1, -1) for n in numbers], axis=1)
    arrays = {
        "x": i["x"], "fside": i["fside_BxSxS2_0"],
        "ctxT": i["ctx_1024"].reshape(B * T, D).T,
        "mask": i["mask_BxS2_ik0"].reshape(1, B * T),
        "Wq": i["L0_xattn_Wq"], "WkT": i["L0_xattn_Wk"].T, "WvT": i["L0_xattn_Wv"].T,
        "bv": i["L0_xattn_bv"].reshape(1, D), "cols": cols, "scalars": scalars,
        "WgsT": i["L0_ffn_Wg_s"].T, "WusT": i["L0_ffn_Wu_s"].T, "WdsT": i["L0_ffn_Wd_s"].T,
        "WgT": i["L0_ffn_Wg"].transpose(0, 2, 1), "WuT": i["L0_ffn_Wu"].transpose(0, 2, 1),
        "WdT": i["L0_ffn_Wd"].transpose(0, 2, 1),
        "WrT": i["L0_ffn_Wr"].T, "rb": i["L0_ffn_rb"].reshape(1, -1),
        "Ws": i["L1_xattn_Ws"], "W": i["L1_xattn_W"],
        "ternT": i["L1_ffn_ternary_weight"].T, "lin_bias": i["L1_ffn_bias"].reshape(1, D),
    }
    nc = bacc.Bacc("TRN2", target_bir_lowering=False, num_devices=1, dynamic_dma_scratch_size=8192)
    feed, args = {}, {}
    for name, v in arrays.items():
        v = np.ascontiguousarray(v)
        feed[f"in_{name}"] = v
        args[name] = nc.dram_tensor(f"in_{name}", v.shape, mybir.dt.from_np(v.dtype), kind="ExternalInput").ap()
    args["out"] = nc.dram_tensor("out", i["x"].shape, F32, kind="ExternalOutput").ap()
    build(nc, args)
    r = run_bass_kernel_spmd(nc, [feed], core_ids=[0])
    return r.results[0]["out"]
```

```python
from contextlib import ExitStack

import concourse.bass as bass
from concourse import mybir

F32 = mybir.dt.float32
BF16 = mybir.dt.bfloat16
I32 = mybir.dt.int32
U32 = mybir.dt.uint32
ALU = mybir.AluOpType
ACT = mybir.ActivationFunctionType
AX = mybir.AxisListType.X

P = 128
LN_EPS = 1e-5
NEG = -1e30
MIN_SCALE = 1e-5
QMAX = 127.0
ROUND = 1.5 * 2 ** 23
FLT_MAX = 3.4028234e38

BIAS_EVERY = 4
GROUPS = [[0], [1, 2], [3, 4], [5, 6], [7]]


class Lane:

    def __init__(self, sem):
        self.sem, self.count, self.ops, self.seen, self.last = sem, 0, [], {}, None

    def wait(self, *tokens):
        for sem, value in tokens:
            if self.seen.get(sem.name, 0) < value:
                self.seen[sem.name] = value
                self.ops.append(lambda e, s=sem, v=value: e.wait_ge(s, v))

    def do(self, instruction, *after):
        self.wait(*after)
        self.count += 1
        self.ops.append(lambda e: instruction(e).then_inc(self.sem, 1))
        self.last = (self.sem, self.count)
        return self.last

    def then(self, instruction, *after):
        return self.do(instruction, self.last, *after)

    def quiet(self, instruction):
        self.ops.append(instruction)

    def dma(self, transfer, gate, *after):
        self.wait(*after)
        gate.count += 16
        self.ops.append(lambda e: transfer(e).then_inc(gate.sem, 16))
        return (gate.sem, gate.count)


class Gate:

    def __init__(self, sem):
        self.sem, self.count = sem, 0

    def token(self):
        return (self.sem, self.count)


class Slot:

    def __init__(self, ap, gate=None):
        self.ap, self.gate, self.free, self.ready = ap, gate, [], None

    def take(self):
        assert self.free is not None, "taken before its last user gave it back"
        tokens, self.free = self.free, None
        return tokens


class Ring:
    def __init__(self, slots):
        self.slots, self.at = slots, -1

    def next(self):
        self.at += 1
        slot = self.slots[self.at % len(self.slots)]
        return slot


def merge(*lists):
    keyed = [((i + 0.5) / len(l), n, i, s) for n, l in enumerate(lists) for i, s in enumerate(l)]
    return [s for _, _, _, s in sorted(keyed, key=lambda k: k[:3])]


def build(nc, a):
    B, S, D = a["x"].shape
    T = a["fside"].shape[2]
    E, _, I = a["WgT"].shape
    DC, IC, ST = D // P, I // P, S // P
    BT = B * T
    SCALE = float(D) ** -0.5
    EW = 2 * DC * I + IC * D
    GT = [len(g) * ST for g in GROUPS]
    RT = [2 * n + E - 1 for n in GT]
    NTM, RTM = max(GT), max(RT)
    assert sum(GROUPS, []) == list(range(B)) and D == 2 * P and T == 64 and S == 512 and I == 512

    ctx = ExitStack()
    with ctx:
        def sb(name, shape, dt=F32):
            return ctx.enter_context(nc.sbuf_tensor(name, shape, dt))

        def sem(name):
            return ctx.enter_context(nc.semaphore(name))

        def gate(name):
            return Gate(sem(name))

        expert_w = sb("expert_w", [P, E, EW])
        shared_w = sb("shared_w", [P, EW])
        stream = Ring([Slot(sb(f"x{i}", [P, ST, D]), gate(f"s_x{i}")) for i in range(6)])
        normT = Slot(sb("normT", [P, DC * S]))
        featT = [Slot(sb(f"featT{c}", [P, S])) for c in range(DC)]
        normed = Ring([Slot(sb(f"normed{i}", [P, D]), gate(f"s_normed{i}")) for i in range(4)])
        wide = Ring([Slot(sb(f"wide{i}", [P, 1024])) for i in range(4)])
        attn_work, out_work = Slot(sb("attn_work", [P, 1024])), Slot(sb("out_work", [P, 1024]))
        act = Ring([Slot(sb(f"act{i}", [P, I])) for i in range(2)])
        actT = Slot(sb("actT", [P, I]))
        rows_in = Ring([Slot(sb(f"rows_in{i}", [P, D]), gate(f"s_rows_in{i}")) for i in range(2)])
        rowsT = Ring([Slot(sb(f"rowsT{i}", [P, D])) for i in range(2)])
        rows_out = Ring([Slot(sb(f"rows_out{i}", [P, D]), gate(f"s_rows_out{i}")) for i in range(2)])
        picked = Ring([Slot(sb(f"picked{i}", [P, D]), gate(f"s_picked{i}")) for i in range(3)])
        score = Slot(sb("score", [P, ST, T]), gate("s_score"))
        rho = sb("rho", [P, ST, T])
        rho_e = sb("rho_e", [P, ST, T])

        txtT = sb("txtT", [P, DC, BT])
        keysq = sb("keysq", [P, DC, BT])
        values = sb("values", [P, B // 2, D])
        feat_w = sb("feat_w", [P, DC, D])
        router_w = sb("router_w", [P, DC, E])
        tern_w = sb("tern_w", [P, DC, D], BF16)
        maskadd = sb("maskadd", [P, BT])
        mulw = sb("mulw", [P, BT])
        addw = sb("addw", [P, BT])
        lin_bias = sb("lin_bias", [P, D])
        pick_w = sb("pick_w", [P, DC, 63])
        row_qb = sb("row_qb", [1, BT])
        row_bv = sb("row_bv", [1, D])
        row_rb = sb("row_rb", [1, E])
        ident = sb("ident", [P, P])
        identb = sb("identb", [P, P], BF16)
        before = sb("before", [P, P])
        ones = sb("ones", [P, P])
        rank8 = sb("rank8", [P, E])
        below = sb("below", [P, E, E])
        steps128 = sb("steps128", [P, NTM])
        tile_id = sb("tile_id", [P, RTM])
        halves = sb("halves", [P, ST])
        cols = sb("cols", [P, 6 * DC])
        scal = sb("scal", [P, 16])
        ln = {k: dict(stats=sb(f"ln_{k}_stats", [P, ST, 6]), mv=sb(f"ln_{k}_mv", [P, NTM, 2]),
                      var=sb(f"ln_{k}_var", [P, ST]), r=sb(f"ln_{k}_r", [P, NTM]),
                      t=sb(f"ln_{k}_t", [P, ST])) for k in ("att", "moe0", "moe1", "mix0", "mix1", "lin")}
        sm = {k: sb(f"sm_{k}", [P, ST]) for k in ("amax", "asum", "rmax", "rsum", "ws", "bs", "A", "B", "t")}
        prob = sb("prob", [P, NTM, E])
        prob2 = sb("prob2", [P, NTM, E])
        hot = [sb(f"hot{k}", [P, NTM, E]) for k in range(2)]
        chosen = sb("chosen", [P, NTM + 1, E])
        posn = sb("posn", [P, NTM + 1, E])
        rt = sb("rt", [P, NTM, E])
        rt2 = sb("rt2", [P, E, E])
        rs = {k: sb(f"rs_{k}", [P, n]) for k, n in
              dict(best=NTM, tiles=E, base=E, pos=NTM, cum=E, eid=RTM).items()}
        cmp_id = sb("cmp_id", [P, RTM, E])
        slot_of = [[sb(f"slot_of{g}{k}", [P, NTM], U32) for k in range(2)] for g in range(2)]
        share = [[sb(f"share{g}{k}", [P, NTM]) for k in range(2)] for g in range(2)]
        owner = [sb(f"owner{g}", [P, RTM], I32) for g in range(2)]

        banks = [Slot(ctx.enter_context(nc.psum_tensor(f"bank{i}", [P, 512], F32))) for i in range(8)]
        up_banks = Ring([(banks[0], banks[1]), (banks[2], banks[3])])
        actT_bank, row_bank, rho_bank = banks[4], banks[5], banks[6]
        misc = Ring([banks[7], banks[0], banks[1], banks[2], banks[3], banks[4], banks[5]])

        rows_dram = [nc.dram_tensor(f"rows_by_expert{g}", (RTM * P, D), F32, kind="Internal").ap() for g in range(2)]
        outs_dram = [nc.dram_tensor(f"expert_rows{g}", (RTM * P, D), F32, kind="Internal").ap() for g in range(2)]

        V, A, PE, G, SP = (Lane(sem(n)) for n in ("s_vector", "s_scalar", "s_tensor", "s_gpsimd", "s_sync"))

        tail = expert_w[:, E - 2:E, :].rearrange("p e n -> p (e n)")
        at = [0]

        def temp(n, dt=F32):
            v = tail[:, at[0]:at[0] + n]
            at[0] += n
            return v.bitcast(dt) if dt is not F32 else v

        ctxT = temp(DC * BT).rearrange("p (c n) -> p c n", c=DC)
        wk, wv, wq, ws = (temp(DC * D).rearrange("p (c n) -> p c n", c=DC) for _ in range(4))
        keysT = temp(DC * BT).rearrange("p (c n) -> p c n", c=DC)
        spread_w = temp(2 * DC * P).rearrange("p (k n) -> p k n", n=P)
        mask_i = temp(BT, I32)
        tern_i = temp(DC * D, I32).rearrange("p (c n) -> p c n", c=DC)
        assert at[0] <= 2 * EW

        def chunked(ap):
            return ap.rearrange("(c p) n -> p c n", p=P)

        g_ctx, g_small, g_late = gate("s_ctx"), gate("s_small"), gate("s_late")
        for dst, src in ((ctxT, chunked(a["ctxT"])), (wk, chunked(a["WkT"])), (wq, chunked(a["Wq"])),
                         (wv, chunked(a["WvT"])), (ws, chunked(a["Ws"]))):
            SP.dma(lambda e, d=dst, s=src: e.dma_start(d, s), g_ctx)
        ctx_in = g_ctx.token()
        BK, TB, WW, CW, CB, BQ = (k * DC for k in range(6))
        GX, GF, BR, ASC, BCW, BCB = 0, 2, 4, 7, 8, 9
        for dst, src in ((cols[:, :], a["cols"]), (row_bv[:, :], a["bv"]), (row_rb[:, :], a["rb"]),
                         (scal[:, 0:10], a["scalars"].to_broadcast([P, 10]))):
            SP.dma(lambda e, d=dst, s=src: e.dma_start(d, s), g_small)
        small_in = g_small.token()

        for m in (ident, identb):
            c = G.do(lambda e, m=m: e.memset(m[:, :], 0.0))
            G.do(lambda e, m=m: e.affine_select(out=m[:, :], in_=m[:, :], compare_op=ALU.not_equal, fill=1.0, base=0,
                                                pattern=[[-1, P]], channel_multiplier=1), c)
        ident_ok = G.last
        c = G.do(lambda e: e.memset(before[:, :], 1.0))
        G.do(lambda e: e.affine_select(out=before[:, :], in_=before[:, :], compare_op=ALU.is_gt, fill=0.0, base=0,
                                       pattern=[[1, P]], channel_multiplier=-1), c)
        G.do(lambda e: e.memset(ones[:, :], 1.0))
        ones_ok = G.last
        G.do(lambda e: e.memset(halves[:, :], -0.5))
        for ap, pattern, base in ((rank8[:, :], [[-1, E]], E), (below[:, :, :], [[1, E], [-1, E]], 0),
                                  (steps128[:, :], [[P, NTM]], 0), (tile_id[:, :], [[1, RTM]], 0)):
            G.do(lambda e, o=ap, p=pattern, b=base: e.iota(o, pattern=p, base=b, channel_multiplier=0,
                                                           allow_small_or_imprecise_dtypes=True))
        consts_ok = G.last
        V.do(lambda e: e.tensor_scalar(below[:, :, :], below[:, :, :], 0.0, None, ALU.is_gt), consts_ok)

        zeros = picked.slots[-1]
        for w in (attn_work, zeros):
            zero_ok = V.do(lambda e, w=w: e.memset(w.ap[:, :], 0.0))
        g_zero = gate("s_zero")

        def zero_rows(r):
            src = zeros.ap[:, :].unsqueeze(1).to_broadcast([P, RTM, D])
            SP.dma(lambda e: e.dma_start(r.rearrange("(n p) d -> p n d", p=P), src), g_zero, zero_ok)
            zeros.free = [g_zero.token()]

        gates_ok = A.do(lambda e: e.activation(scal[:, GX:GX + 4], scal[:, GX:GX + 4], ACT.Tanh), small_in)
        V.wait(gates_ok)
        GX0, GX1, GF0, GF1 = (scal[:, k:k + 1] for k in (GX, GX + 1, GF, GF + 1))
        V.do(lambda e: e.tensor_tensor(scal[:, BR:BR + 1], scal[:, BR:BR + 1], scal[:, BR + 1:BR + 2], ALU.add))
        V.then(lambda e: e.tensor_tensor(scal[:, BR:BR + 1], scal[:, BR:BR + 1], scal[:, BR + 2:BR + 3], ALU.subtract))
        side_w = scal[:, BR:BR + 1]
        V.do(lambda e: e.tensor_scalar(scal[:, ASC:ASC + 1], scal[:, ASC:ASC + 1], MIN_SCALE, FLT_MAX, ALU.max, ALU.min))
        V.then(lambda e: e.reciprocal(scal[:, 10:11], scal[:, ASC:ASC + 1]))
        V.do(lambda e: e.tensor_tensor(scal[:, 11:12], scal[:, ASC:ASC + 1], GF1, ALU.mult))
        inv_step, gated_step = scal[:, 10:11], scal[:, 11:12]
        c = V.do(lambda e: e.memset(pick_w[:, :, :], 0.0))
        for k in range(DC):
            V.do(lambda e, k=k: e.tensor_copy(pick_w[:, k, 31:32], cols[:, WW + k:WW + k + 1]), c)
        for k in range(2 * DC):
            V.do(lambda e, k=k: e.tensor_copy(spread_w[:, k, :], cols[:, CW + k:CW + k + 1].to_broadcast([P, P])))
        prep_ok = V.last

        def bank_for(pe=PE):
            b = misc.next()
            PE.wait(*b.take())
            return b

        def project(out, lhs, rhs, n, bias=None, row=None, parts=P):
            b = bank_for()
            for c in range(DC):
                stop = c == DC - 1 and row is None
                f = lambda e, c=c, stop=stop: e.matmul(b.ap[0:parts, 0:n], lhs(c), rhs(c), start=c == 0, stop=stop)
                done = PE.do(f) if stop else PE.quiet(f)
            if row is not None:
                done = PE.do(lambda e: e.matmul(b.ap[0:parts, 0:n], ones[0:1, 0:parts], row, start=False, stop=True))
            if bias is None:
                b.free = [A.do(lambda e: e.activation(out, b.ap[0:parts, 0:n], ACT.Copy), done)]
            else:
                b.free = [V.do(lambda e: e.tensor_scalar(out, b.ap[0:parts, 0:n], bias, None, ALU.add), done)]

        PE.wait(ctx_in, small_in, ident_ok, ones_ok, prep_ok)
        for o in range(DC):
            project(keysT[:, o, :], lambda c, o=o: wk[:, c, o * P:(o + 1) * P], lambda c: ctxT[:, c, :], BT,
                    bias=cols[:, BK + o:BK + o + 1])
        PE.wait(V.last)
        for o in range(DC):
            project(keysq[:, o, :], lambda c, o=o: wq[:, c, o * P:(o + 1) * P], lambda c: keysT[:, c, :], BT)
        project(row_qb[0:1, :], lambda c: cols[:, BQ + c:BQ + c + 1], lambda c: keysT[:, c, :], BT, parts=1)
        for j in range(B // 2):
            project(values[:, j, :], lambda c, j=j: ctxT[:, c, 2 * T * j:2 * T * (j + 1)], lambda c: wv[:, c, :], D,
                    row=row_bv[0:1, :])
        attn_ready = [A.last]

        def late_prologue():
            for dst, src in ((feat_w[:, :, :], chunked(a["W"])), (router_w[:, :, :], chunked(a["WrT"])),
                             (tern_i, chunked(a["ternT"])), (lin_bias[:, :], a["lin_bias"].to_broadcast([P, D])),
                             (mask_i, a["mask"].to_broadcast([P, BT]))):
                SP.dma(lambda e, d=dst, s=src: e.dma_start(d, s), g_late)
            late_in = g_late.token()
            for o in range(DC):
                project(txtT[:, o, :], lambda c, o=o: ws[:, c, o * P:(o + 1) * P], lambda c: ctxT[:, c, :], BT,
                        bias=cols[:, TB + o:TB + o + 1])
            project(mulw[:, :], lambda c: spread_w[:, c, :], lambda c: ctxT[:, c, :], BT)
            project(addw[:, :], lambda c: spread_w[:, DC + c, :], lambda c: ctxT[:, c, :], BT)
            V.do(lambda e: e.tensor_scalar(tern_w[:, :, :], tern_i, 1.0, None, ALU.subtract), late_in)
            V.do(lambda e: e.tensor_scalar(maskadd[:, :], mask_i, -1.0, 1.0, ALU.mult, ALU.add))
            V.then(lambda e: e.tensor_scalar(maskadd[:, :], maskadd[:, :], NEG, None, ALU.mult))
            V.do(lambda e: e.tensor_scalar(lin_bias[:, :], lin_bias[:, :], GF1, None, ALU.mult))
            PE.wait(late_in)

        g_exp = gate("s_experts")

        def load_expert(dst, WgT, WuT, WdT, *after):
            n = DC * I
            for lo, src, rows in ((0, WgT, n), (n, WuT, n), (2 * n, WdT, IC * D)):
                inner = I if src is not WdT else D
                SP.dma(lambda e, lo=lo, s=src, r=rows, i=inner: e.dma_start(
                    dst[:, lo:lo + r].rearrange("p (c n) -> p c n", n=i), chunked(s)), g_exp, *after)

        def norm_stats(k, x, ok, first=0):
            s, st = ln[k], {}
            var, r, t = s["var"][:, :], s["r"][:, first:first + ST], s["t"][:, :]

            def stats():
                for i in range(ST):
                    V.do(lambda e, i=i: e.bn_stats(s["stats"][:, i, :], x[:, i, :]))

            def aggregate():
                V.wait(V.last)
                for i in range(ST):
                    V.do(lambda e, i=i: e.bn_aggr(s["mv"][:, first + i, :], s["stats"][:, i, :]))

            def power():
                c = V.then(lambda e: e.tensor_scalar(var, s["mv"][:, first:first + ST, 1], LN_EPS, None, ALU.add))
                st["r"] = G.do(lambda e: e.tensor_tensor(r, var, halves[:, :], ALU.pow), c)

            def newton():
                V.do(lambda e: e.tensor_tensor(t, r, r, ALU.mult), st["r"])
                V.then(lambda e: e.tensor_tensor(t, t, var, ALU.mult))
                V.then(lambda e: e.tensor_scalar(t, t, -0.5, 1.5, ALU.mult, ALU.add))
                ok[0] = V.then(lambda e: e.tensor_tensor(r, r, t, ALU.mult))
            return [stats, aggregate, power, newton]

        def normalize(k, x, i, at, stats_ok):
            s, slot = ln[k], normed.next()
            slot.ready = V.do(lambda e: e.tensor_scalar(slot.ap[:, :], x[:, i, :], s["mv"][:, at, 0:1], s["r"][:, at:at + 1],
                                                        ALU.subtract, ALU.mult), stats_ok, *slot.take())
            slot.free = []
            return slot

        def chunks(slot):
            return slot.ap[:, :].rearrange("p (c n) -> p c n", c=DC)

        def transpose_norm(k, x, first, stats_ok, box, target):
            def pair(h):
                def step():
                    slots = [normalize(k, x, i, first + i, stats_ok[0]) for i in (2 * h, 2 * h + 1)]
                    b = bank_for()
                    for n, slot in enumerate(slots):
                        PE.wait(slot.ready)
                        for c in range(DC):
                            f = lambda e, n=n, c=c, s=slot: e.transpose(b.ap[:, (n * DC + c) * P:(n * DC + c + 1) * P],
                                                                        s.ap[:, c * P:(c + 1) * P], ident[:, :])
                            done = PE.do(f) if c == DC - 1 else PE.quiet(f)
                        slot.free = [done]
                    out = chunks(target).rearrange("p c (i n) -> p i c n", n=P)[:, 2 * h:2 * h + 2, :, :]
                    b.free = [V.do(lambda e: e.tensor_copy(out, b.ap[:, :].rearrange("p (i c n) -> p i c n", i=2, c=DC)),
                                   done, *(target.take() if h == 0 else []))]
                    box[:] = [V.last]
                return step
            return [pair(0), pair(1)]

        xs = {}
        moe_ok = {}

        def attend(b):
            st = {}
            gi = next(i for i, g in enumerate(GROUPS) if b in g)
            first = GROUPS[gi].index(b) * ST
            key = f"moe{gi % 2}"
            half = (b % 2) * T
            stats1, stats2, lnT1, lnT2 = [None], [None], [], []

            def load():
                x = xs[b] = stream.next()
                x.ready = SP.dma(lambda e: e.dma_start(x.ap[:, :, :], a["x"][b].rearrange("(i p) d -> p i d", p=P)),
                                 x.gate, *x.take())
                st["side"] = SP.dma(lambda e: e.dma_start(score.ap[:, :, :], a["fside"][b].rearrange("(i p) d -> p i d", p=P)),
                                    score.gate, *score.take())

            def arrived():
                V.wait(xs[b].ready)
                V.do(lambda e: e.tensor_scalar(score.ap[:, :, :], score.ap[:, :, :], side_w, None, ALU.mult), st["side"])

            def scores():
                bk = bank_for()
                PE.wait(*lnT1, *attn_ready)
                for i in range(ST):
                    o = bk.ap[:, i * T:(i + 1) * T]
                    PE.quiet(lambda e, o=o: e.matmul(o, ones[0:1, :], row_qb[0:1, b * T:(b + 1) * T], start=True, stop=False))
                    for c in range(DC):
                        f = lambda e, o=o, c=c, i=i: e.matmul(o, normT.ap[:, c * S + i * P:c * S + (i + 1) * P],
                                                              keysq[:, c, b * T:(b + 1) * T], start=False, stop=c == DC - 1)
                        done = PE.do(f) if c == DC - 1 and i == ST - 1 else PE.quiet(f)
                normT.free = [done]
                sc = score.ap
                bk.free = [V.do(lambda e: e.scalar_tensor_tensor(out=sc[:, :, :], in0=bk.ap[:, 0:ST * T].rearrange("p (i t) -> p i t", t=T),
                                                                 scalar=SCALE, in1=sc[:, :, :], op0=ALU.mult, op1=ALU.add), V.last, done)]

            def softmax():
                sc, m = score.ap, sm["amax"]
                V.then(lambda e: e.tensor_reduce(m[:, :], sc[:, :, :], AX, ALU.max))
                V.then(lambda e: e.tensor_tensor(sc[:, :, :], sc[:, :, :], m[:, :].unsqueeze(2).to_broadcast([P, ST, T]), ALU.subtract))
                w = st["w"] = attn_work
                ex = st["ex"] = w.ap[:, 0:ST * P].rearrange("p (i t) -> p i t", t=P)[:, :, half:half + T]
                st["e"] = A.do(lambda e: e.activation(ex, sc[:, :, :], ACT.Exp), V.last, *w.take())
                score.free = [st["e"]]

            def sums():
                V.do(lambda e: e.tensor_reduce(sm["asum"][:, :], st["ex"], AX, ALU.add), st["e"])
                V.then(lambda e: e.reciprocal(sm["asum"][:, :], sm["asum"][:, :]))
                st["sum"] = V.then(lambda e: e.tensor_scalar(sm["asum"][:, :], sm["asum"][:, :], GX0, None, ALU.mult))

            def turn():
                bk, w = bank_for(), st["w"]
                PE.wait(st["e"])
                for i in range(ST):
                    f = lambda e, i=i: e.transpose(bk.ap[:, i * P:(i + 1) * P], w.ap[:, i * P:(i + 1) * P], ident[:, :])
                    done = PE.do(f) if i == ST - 1 else PE.quiet(f)
                st["eT"] = A.do(lambda e: e.activation(w.ap[:, 512:1024], bk.ap[:, :], ACT.Copy), done)
                bk.free = [st["eT"]]

            def weigh(h):
                def step():
                    bk, w, x = bank_for(), st["w"], xs[b].ap
                    PE.wait(st["eT"])
                    for n in range(2):
                        i = 2 * h + n
                        f = lambda e, i=i, n=n: e.matmul(bk.ap[:, n * D:(n + 1) * D], w.ap[half:half + T, 512 + i * P:512 + (i + 1) * P],
                                                         values[half:half + T, b // 2, :], start=True, stop=True)
                        done = PE.do(f) if n else PE.quiet(f)
                    if h == 1:
                        w.free = [done]
                    for n in range(2):
                        i = 2 * h + n
                        V.do(lambda e, i=i, n=n: e.scalar_tensor_tensor(
                            out=x[:, i, :], in0=bk.ap[:, n * D:(n + 1) * D], scalar=sm["asum"][:, i:i + 1], in1=x[:, i, :],
                            op0=ALU.mult, op1=ALU.add), done, st["sum"])
                    bk.free = [V.last]
                return step

            def attended():
                V.wait(V.last)

            def normed_moe():
                moe_ok[b] = stats2[0]

            def logits():
                bk = bank_for()
                PE.wait(*lnT2)
                for i in range(ST):
                    o = bk.ap[:, i * E:(i + 1) * E]
                    PE.quiet(lambda e, o=o: e.matmul(o, ones[0:1, :], row_rb[0:1, :], start=True, stop=False))
                    for c in range(DC):
                        f = lambda e, o=o, c=c, i=i: e.matmul(o, normT.ap[:, c * S + i * P:c * S + (i + 1) * P], router_w[:, c, :],
                                                              start=False, stop=c == DC - 1)
                        done = PE.do(f) if c == DC - 1 and i == ST - 1 else PE.quiet(f)
                normT.free = [done]
                pr = prob[:, first:first + ST, :]
                bk.free = [A.do(lambda e: e.activation(pr, bk.ap[:, 0:ST * E].rearrange("p (i n) -> p i n", n=E), ACT.Exp, scale=-1.0),
                                done, *prob_free)]
                st["p"] = A.last

            def sigmoid():
                pr = prob[:, first:first + ST, :]
                V.do(lambda e: e.tensor_scalar(pr, pr, 1.0, None, ALU.add), st["p"])
                V.then(lambda e: e.reciprocal(pr, pr))

            x = _Later(xs, b)
            return ([load, arrived] + norm_stats("att", x, stats1) + transpose_norm("att", x, 0, stats1, lnT1, normT)
                    + [scores, softmax, sums, turn, weigh(0), weigh(1), attended] + norm_stats(key, x, stats2, first)
                    + [normed_moe] + transpose_norm(key, x, first, stats2, lnT2, normT) + [logits, sigmoid])

        prob_free = []

        def route(gi):
            par, n, R, group = gi % 2, GT[gi], RT[gi], GROUPS[gi]
            pr, p2, ch, rb = prob[:, 0:n, :], prob2[:, 0:n, :], chosen[:, 0:n, :], rt[:, 0:n, :]
            best = rs["best"][:, 0:n]

            def wide_(v):
                return v.unsqueeze(2).to_broadcast([P, n, E])

            def choose(k):
                rank = rank8[:, :].unsqueeze(1).to_broadcast([P, n, E])

                def step():
                    src, top, h = (pr, p2)[k], share[par][k][:, 0:n], hot[k][:, 0:n, :]
                    V.then(lambda e, s=src, t=top: e.tensor_reduce(t, s, AX, ALU.max))
                    V.then(lambda e, s=src, t=top: e.tensor_tensor(rb, s, wide_(t), ALU.is_equal))
                    V.then(lambda e: e.tensor_tensor(rb, rb, rank, ALU.mult))
                    V.then(lambda e: e.tensor_reduce(best, rb, AX, ALU.max))
                    V.then(lambda e, h=h: e.tensor_tensor(h, rank, wide_(best), ALU.is_equal))
                    if k == 0:
                        V.then(lambda e, h=h: e.scalar_tensor_tensor(out=p2, in0=h, scalar=-2.0, in1=pr, op0=ALU.mult, op1=ALU.add))
                return step

            def choice():
                prob_free[:] = [V.last]
                V.then(lambda e: e.tensor_tensor(ch, hot[0][:, 0:n, :], hot[1][:, 0:n, :], ALU.add))
                V.do(lambda e: e.memset(chosen[:, n, :], 0.0))
                for k in range(2):
                    V.do(lambda e, k=k: e.tensor_scalar(share[par][k][:, 0:n], share[par][k][:, 0:n], GF0, None, ALU.mult))

            def count():
                bk = bank_for()
                PE.wait(V.last, consts_ok)
                W = (n + 1) * E
                PE.quiet(lambda e: e.matmul(bk.ap[:, 0:W], before[:, :], chosen[:, 0:n + 1, :].rearrange("p i e -> p (i e)"), start=True, stop=False))
                for i in range(n):
                    m = n - i
                    f = lambda e, i=i, m=m: e.matmul(bk.ap[:, (i + 1) * E:W].rearrange("p (j e) -> p j e", e=E), ones[:, :],
                                                     chosen[:, i:i + 1, :].to_broadcast([P, m, E]), start=False, stop=i == n - 1)
                    done = PE.do(f) if i == n - 1 else PE.quiet(f)
                bk.free = [V.do(lambda e: e.tensor_copy(posn[:, 0:n + 1, :].rearrange("p i e -> p (i e)"), bk.ap[:, 0:W]), done)]

            def place():
                total = posn[:, n, :]
                t2 = rt2[:, :, :]
                tiles, base, cum = (rs[k][:, :] for k in ("tiles", "base", "cum"))
                V.then(lambda e: e.tensor_tensor(rt[:, 0:n, :].rearrange("p j e -> p e j"), total.unsqueeze(2).to_broadcast([P, E, n]),
                                                 steps128[:, 0:n].unsqueeze(1).to_broadcast([P, E, n]), ALU.is_gt))
                V.then(lambda e: e.tensor_reduce(tiles, rt[:, 0:n, :].rearrange("p j e -> p e j"), AX, ALU.add))
                V.then(lambda e: e.tensor_tensor(t2, below[:, :, :], tiles.unsqueeze(1).to_broadcast([P, E, E]), ALU.mult))
                V.then(lambda e: e.tensor_reduce(base, t2, AX, ALU.add))
                V.then(lambda e: e.tensor_tensor(cum, base, tiles, ALU.add))
                V.then(lambda e: e.tensor_scalar(base, base, float(P), None, ALU.mult))

            def place_rows():
                pos, base = posn[:, 0:n, :], rs["base"][:, :]
                V.then(lambda e: e.tensor_tensor(pos, pos, base.unsqueeze(1).to_broadcast([P, n, E]), ALU.add))
                for k in range(2):
                    V.then(lambda e, k=k: e.tensor_tensor(rb, hot[k][:, 0:n, :], pos, ALU.mult))
                    V.then(lambda e: e.tensor_reduce(rs["pos"][:, 0:n], rb, AX, ALU.add))
                    V.then(lambda e, k=k: e.tensor_copy(slot_of[par][k][:, 0:n], rs["pos"][:, 0:n]), *gathers_done[par])

            def place_owners():
                cum = rs["cum"][:, :]
                cm = cmp_id[:, 0:R, :]
                V.then(lambda e: e.tensor_tensor(cm, cum.unsqueeze(1).to_broadcast([P, R, E]),
                                                 tile_id[:, 0:R].unsqueeze(2).to_broadcast([P, R, E]), ALU.is_le))
                V.then(lambda e: e.tensor_reduce(rs["eid"][:, 0:R], cm, AX, ALU.add))
                placed[gi] = V.then(lambda e: e.tensor_scalar(owner[par][:, 0:R], rs["eid"][:, 0:R], float(E - 1), None, ALU.min),
                                    *owner_free[par])

            def scatter(i):
                def step():
                    b, key = group[i // ST], f"moe{par}"
                    slot = normalize(key, xs[b].ap, i % ST, i, moe_ok[b])
                    for k in range(2):
                        tok = G.dma(lambda e, k=k: e.indirect_dma_start(
                            out=rows_dram[par], out_offset=bass.IndirectOffsetOnAxis(ap=slot_of[par][k][:, i:i + 1], axis=0),
                            in_=slot.ap[:, :], in_offset=None), slot.gate, slot.ready, placed[gi], *rows_free[par],
                            g_zero.token())
                    slot.free = [tok]
                    scattered.setdefault(gi, {})[slot.gate.sem.name] = tok
                return step

            return [choose(0), choose(1), choice, count, place, place_rows, place_owners] + [scatter(i) for i in range(n)]

        placed, scattered = {}, {}
        gathers_done = [[], []]
        owner_free = [[], []]
        rows_free = [[], []]

        tiles = [(gi, "shared", i) for gi in range(len(GROUPS)) for i in range(GT[gi])]
        tiles = []
        for gi in range(len(GROUPS)):
            tiles += [(gi, "shared", i) for i in range(GT[gi])] + [(gi, "routed", s) for s in range(RT[gi])]
        work = {}
        stored = {}

        def fetch(n):
            if n >= len(tiles) or tiles[n][1] != "routed":
                return
            gi, _, s = tiles[n]
            r = work.setdefault(n, {})["rows"] = rows_in.next()
            r.ready = SP.dma(lambda e: e.dma_start(r.ap[:, :], rows_dram[gi % 2][s * P:(s + 1) * P, :]), r.gate,
                             *r.take(), *scattered[gi].values())

        def turn_rows(n):
            if n >= len(tiles):
                return
            gi, kind, s = tiles[n]
            w = work.setdefault(n, {})
            if kind == "routed":
                r = w["rows"]
                w["owner_ok"] = placed[gi]
            else:
                b = GROUPS[gi][s // ST]
                r = normalize(f"moe{gi % 2}", xs[b].ap, s % ST, s, moe_ok[b])
            PE.wait(r.ready, *row_bank.take())
            for c in range(DC):
                f = lambda e, c=c: e.transpose(row_bank.ap[:, c * P:(c + 1) * P], r.ap[:, c * P:(c + 1) * P], ident[:, :])
                done = PE.do(f) if c == DC - 1 else PE.quiet(f)
            r.free = [done]
            if kind == "routed":
                rows_free[gi % 2] = [done]
            w["rows_ok"] = done

        def copy_rows(n):
            if n >= len(tiles):
                return
            w = work[n]
            t = w["lhsT"] = rowsT.next()
            w["rowsT"] = V.do(lambda e: e.tensor_copy(t.ap[:, :], row_bank.ap[:, 0:D]), w["rows_ok"], *t.take())
            row_bank.free = [w["rowsT"]]

        N1 = DC * I

        def gate_products(n):
            gi, kind, s = tiles[n]
            w = work[n]
            w["banks"] = up_banks.next()
            PE.wait(w["rowsT"], experts_in[0])
            if kind == "routed":
                PE.wait(w["owner_ok"])

                def load_owner(e):
                    w["e"] = e.value_load(owner[gi % 2][0:1, s:s + 1], min_val=0, max_val=E - 1)
                PE.quiet(load_owner)
            weights = expert_w[:, :, :].rearrange("p e n -> p (e n)")
            w["rhs"] = lambda lo, m: (shared_w[:, lo:lo + m] if kind == "shared"
                                      else weights[:, bass.ds(w["e"] * EW + lo, m)])
            w["gate_ok"] = products(w, w["banks"][0], 0)

        def up_products(n):
            w = work[n]
            w["up_ok"] = products(w, w["banks"][1], N1)
            w["lhsT"].free = [w["up_ok"]]

        def products(w, bank, lo):
            PE.wait(*bank.take())
            t = w["lhsT"].ap
            for c in range(DC):
                f = lambda e, c=c: e.matmul(bank.ap[:, :], t[:, c * P:(c + 1) * P], w["rhs"](lo + c * I, I), start=c == 0, stop=c == DC - 1)
                done = PE.do(f) if c == DC - 1 else PE.quiet(f)
            return done

        def gate_act(n):
            w = work[n]
            bg, bu = w["banks"]
            h = w["act"] = act.next()
            t = A.do(lambda e: e.activation(h.ap[:, :], bg.ap[:, :], ACT.Tanh, scale=0.5), w["gate_ok"], *h.take())
            V.do(lambda e: e.scalar_tensor_tensor(out=h.ap[:, :], in0=h.ap[:, :], scalar=1.0, in1=bg.ap[:, :],
                                                  op0=ALU.add, op1=ALU.mult), t)
            w["h"] = V.then(lambda e: e.scalar_tensor_tensor(out=h.ap[:, :], in0=h.ap[:, :], scalar=0.5, in1=bu.ap[:, :],
                                                             op0=ALU.mult, op1=ALU.mult), w["up_ok"])
            bg.free = bu.free = [w["h"]]

        def turn_act(n):
            w = work[n]
            h = w["act"]
            PE.wait(w["h"], *actT_bank.take())
            for c in range(IC):
                f = lambda e, c=c: e.transpose(actT_bank.ap[:, c * P:(c + 1) * P], h.ap[:, c * P:(c + 1) * P], ident[:, :])
                done = PE.do(f) if c == IC - 1 else PE.quiet(f)
            h.free = [done]
            w["turned"] = done

        def copy_act(n):
            w = work[n]
            w["actT"] = A.do(lambda e: e.activation(actT.ap[:, :], actT_bank.ap[:, :], ACT.Copy), w["turned"], *actT.take())
            actT_bank.free = [w["actT"]]

        def narrow(n):
            gi, kind, s = tiles[n]
            w = work[n]
            PE.wait(w["actT"], *row_bank.take())
            for c in range(IC):
                f = lambda e, c=c: e.matmul(row_bank.ap[:, 0:D], actT.ap[:, c * P:(c + 1) * P],
                                            w["rhs"](2 * N1 + c * D, D), start=c == 0, stop=c == IC - 1)
                done = PE.do(f) if c == IC - 1 else PE.quiet(f)
            actT.free = [done]
            w["done"] = done
            if kind == "routed" and s == RT[gi] - 1:
                owner_free[gi % 2] = [done]

        def add_or_store(n):
            gi, kind, s = tiles[n]
            done = work.pop(n)["done"]
            if kind == "shared":
                x = xs[GROUPS[gi][s // ST]].ap[:, s % ST, :]
                row_bank.free = [V.do(lambda e: e.scalar_tensor_tensor(out=x, in0=row_bank.ap[:, 0:D], scalar=GF0, in1=x,
                                                                       op0=ALU.mult, op1=ALU.add), done)]
            else:
                y = rows_out.next()
                row_bank.free = [V.do(lambda e: e.tensor_copy(y.ap[:, :], row_bank.ap[:, 0:D]), done, *y.take())]
                tok = SP.dma(lambda e: e.dma_start(outs_dram[gi % 2][s * P:(s + 1) * P, :], y.ap[:, :]), y.gate,
                             row_bank.free[0], *gathers_done[gi % 2])
                y.free = [tok]
                stored.setdefault(gi, {})[y.gate.sem.name] = tok

        def expert_steps(gi):
            lo = sum(GT[:gi]) + sum(RT[:gi])
            hi = lo + GT[gi] + RT[gi]
            last = hi == len(tiles)
            steps = []
            for n in range(lo, hi + last):
                def gate_step(n=n):
                    if n == lo and n not in work:
                        turn_rows(n)
                        copy_rows(n)
                    if n < len(tiles):
                        gate_products(n)

                def turn_step(n=n):
                    if n - 1 in work:
                        turn_act(n - 1)
                        copy_act(n - 1)
                    if n + 1 < hi:
                        turn_rows(n + 1)
                        copy_rows(n + 1)
                    for m in ([n + 3] if n > lo else [n + 1, n + 2, n + 3]):
                        if m < hi:
                            fetch(m)

                def up_step(n=n):
                    if n < len(tiles):
                        up_products(n)

                def down_step(n=n):
                    if n - 1 in work:
                        narrow(n - 1)
                        add_or_store(n - 1)
                    if n < len(tiles):
                        gate_act(n)
                steps += [gate_step, turn_step, up_step, down_step]
            return steps

        def mix_in(b):
            gi = next(i for i, g in enumerate(GROUPS) if b in g)
            first, par = GROUPS[gi].index(b) * ST, gi % 2
            stats, lnT = [None], mixT[b]

            waiting = []

            def gather(i, k):
                def step():
                    y = picked.next()
                    y.ready = G.dma(lambda e: e.indirect_dma_start(
                        out=y.ap[:, :], out_offset=None, in_=outs_dram[par][0:RT[gi] * P, :],
                        in_offset=bass.IndirectOffsetOnAxis(ap=slot_of[par][k][:, first + i:first + i + 1], axis=0)),
                        y.gate, *stored[gi].values(), *y.take())
                    waiting.append((i, k, y))
                return step

            def add():
                i, k, y = waiting.pop(0)
                x = xs[b].ap[:, i, :]
                y.free = gathers_done[par] = [V.do(lambda e: e.scalar_tensor_tensor(
                    out=x, in0=y.ap[:, :], scalar=share[par][k][:, first + i:first + i + 1], in1=x,
                    op0=ALU.mult, op1=ALU.add), V.last, y.ready)]
            order = [gather(i, k) for i in range(ST) for k in range(2)]
            ahead = len(picked.slots)
            steps = order[:ahead]
            for g in order[ahead:]:
                steps += [add, g]
            steps += [add] * ahead + [lambda: V.wait(V.last)]
            x = _Later(xs, b)
            return (steps + norm_stats(f"mix{b % 2}", x, stats)
                    + transpose_norm(f"mix{b % 2}", x, 0, stats, lnT, out_work))

        feat_read = [[], []]
        on_scalar_too = [True]
        mixT = {b: [] for b in range(B)}
        feat_ok = {}

        def feature(b, ec):
            def step():
                bk = bank_for()
                PE.wait(*mixT[b])
                for c in range(DC):
                    f = lambda e, c=c: e.matmul(bk.ap[:, :], feat_w[:, c, ec * P:(ec + 1) * P], out_work.ap[:, c * S:(c + 1) * S],
                                                start=c == 0, stop=c == DC - 1)
                    done = PE.do(f) if c == DC - 1 else PE.quiet(f)
                if ec == DC - 1:
                    out_work.free = [done]
                feat_ok[b, ec] = V.do(lambda e: e.tensor_copy(featT[ec].ap[:, :], bk.ap[:, :]), done, *feat_read[ec])
                bk.free = [feat_ok[b, ec]]
            return step

        LAG = len(wide.slots) - 1
        H = S // 2
        pending = []

        def sum_unit(u):
            b, ec, m, w, ready = u
            PE.wait(ready)
            if (ec, m) == (0, 0):
                PE.wait(*rho_bank.take())
            for j in range(4):
                f = lambda e, j=j: e.matmul(rho_bank.ap[32 * j:32 * j + 32, 0:H], pick_w[:, ec, 31 - m:63 - m],
                                            w.ap[:, j * H:(j + 1) * H], start=(ec, m) == (0, 0), stop=(ec, m) == (DC - 1, T // 2 - 1))
                done = PE.do(f) if j == 3 else PE.quiet(f)
            w.free = [done]
            rho_done[b] = done

        rho_done = {}

        def tanh_steps(b, ec):
            def unit(m):
                def step():
                    w = wide.next()
                    free = w.take()
                    on_scalar = on_scalar_too[0] and m % BIAS_EVERY == 0
                    for n in range(2):
                        t = b * T + 2 * m + n
                        z, f, c = w.ap[:, n * S:(n + 1) * S], featT[ec].ap[:, :], txtT[:, ec, t:t + 1]
                        if on_scalar:
                            ready = A.do(lambda e, z=z, f=f, c=c: e.activation(z, f, ACT.Tanh, bias=c), feat_ok[b, ec], *free)
                        else:
                            V.do(lambda e, z=z, f=f, c=c: e.tensor_scalar(z, f, c, None, ALU.add), feat_ok[b, ec], *free)
                    if on_scalar:
                        feat_read[ec] = [ready]
                    else:
                        ready = A.do(lambda e: e.activation(w.ap[:, :], w.ap[:, :], ACT.Tanh), V.last)
                    pending.append((b, ec, m, w, ready))
                    if len(pending) > LAG:
                        sum_unit(pending.pop(0))
                return step
            steps = [unit(m) for m in range(T // 2)]
            if ec == DC - 1:
                def flush():
                    while pending:
                        sum_unit(pending.pop(0))
                steps.append(flush)
            return steps

        def mix_out(b):
            st = {}
            stats4, x = [None], _Later(xs, b)

            def scores():
                w = st["w"] = out_work
                st["ev"] = V.do(lambda e: e.tensor_copy(w.ap[:, 0:H], rho_bank.ap[:, 0:H]), rho_done[b], *w.take())
                rho_bank.free = [st["ev"]]

            def turn():
                w, bk = st["w"], bank_for()
                PE.wait(st["ev"])
                for k in range(2):
                    f = lambda e, k=k: e.transpose(bk.ap[:, k * P:(k + 1) * P], w.ap[:, k * P:(k + 1) * P], ident[:, :])
                    done = PE.do(f) if k else PE.quiet(f)
                w.free = [done]
                tiles_of = rho[:, :, :].rearrange("p (h k) (m t) -> p k h t m", k=2, t=2)
                mask = maskadd[:, b * T:(b + 1) * T].rearrange("p (m t) -> p t m", t=2).unsqueeze(1).to_broadcast([P, 2, 2, T // 2])
                for k in range(2):
                    V.do(lambda e, k=k: e.tensor_tensor(
                        tiles_of[:, k, :, :, :], bk.ap[:, k * P:(k + 1) * P].rearrange("p (t h m) -> p h t m", t=2, h=2), mask, ALU.add), done)
                bk.free = [V.last]

            def softmax():
                V.then(lambda e: e.tensor_reduce(sm["rmax"][:, :], rho[:, :, :], AX, ALU.max))
                V.then(lambda e: e.tensor_tensor(rho[:, :, :], rho[:, :, :], sm["rmax"][:, :].unsqueeze(2).to_broadcast([P, ST, T]),
                                                 ALU.subtract))
                st["e"] = A.do(lambda e: e.activation(rho_e[:, :, :], rho[:, :, :], ACT.Exp), V.last)

            def weigh():
                V.do(lambda e: e.tensor_reduce(sm["rsum"][:, :], rho_e[:, :, :], AX, ALU.add), st["e"])
                V.then(lambda e: e.reciprocal(sm["rsum"][:, :], sm["rsum"][:, :]))

            def weigh_with(out, vec):
                def step():
                    cv = vec[:, b * T:(b + 1) * T].unsqueeze(1).to_broadcast([P, ST, T])
                    V.then(lambda e: e.tensor_tensor(rho[:, :, :], rho_e[:, :, :], cv, ALU.mult))
                    V.then(lambda e: e.tensor_reduce(sm[out][:, :], rho[:, :, :], AX, ALU.add))
                    V.then(lambda e: e.tensor_tensor(sm[out][:, :], sm[out][:, :], sm["rsum"][:, :], ALU.mult))
                return step

            def squash():
                A.do(lambda e: e.activation(sm["ws"][:, :], sm["ws"][:, :], ACT.Tanh, bias=scal[:, BCW:BCW + 1]), V.last)
                st["wb"] = A.do(lambda e: e.activation(sm["bs"][:, :], sm["bs"][:, :], ACT.Tanh, bias=scal[:, BCB:BCB + 1]))

            def apply():
                own = ln[f"mix{b % 2}"]
                r, mean, Ac, Bc = own["r"][:, 0:ST], own["mv"][:, 0:ST, 0], sm["A"][:, :], sm["B"][:, :]
                V.do(lambda e: e.tensor_tensor(Ac, sm["ws"][:, :], r, ALU.mult), st["wb"])
                V.then(lambda e: e.tensor_scalar(Ac, Ac, GX1, None, ALU.mult))
                V.then(lambda e: e.tensor_tensor(sm["t"][:, :], Ac, mean, ALU.mult))
                V.then(lambda e: e.scalar_tensor_tensor(out=Bc, in0=sm["bs"][:, :], scalar=GX1, in1=sm["t"][:, :],
                                                        op0=ALU.mult, op1=ALU.subtract))
                V.then(lambda e: e.tensor_scalar(Ac, Ac, 1.0, None, ALU.add))

            def apply_to_x():
                V.wait(V.last)
                for i in range(ST):
                    V.do(lambda e, i=i: e.tensor_scalar(x.ap[:, i, :], x.ap[:, i, :], sm["A"][:, i:i + 1], sm["B"][:, i:i + 1],
                                                        ALU.mult, ALU.add))
                V.wait(V.last)

            def quantize(i):
                def step():
                    s, o = normalize("lin", x.ap, i, i, stats4[0]), normed.next()
                    q = out_work.ap[:, S:2 * S].bitcast(BF16)[:, i * D:(i + 1) * D]
                    V.then(lambda e: e.tensor_scalar(o.ap[:, :], s.ap[:, :], inv_step, 0.0, ALU.mult, ALU.max), *o.take())
                    V.do(lambda e: e.tensor_scalar(s.ap[:, :], s.ap[:, :], inv_step, 0.0, ALU.mult, ALU.min))
                    V.then(lambda e: e.tensor_tensor(s.ap[:, :], s.ap[:, :], o.ap[:, :], ALU.add))
                    V.then(lambda e: e.tensor_scalar(s.ap[:, :], s.ap[:, :], QMAX, -QMAX, ALU.min, ALU.max))
                    V.then(lambda e: e.tensor_scalar(q, s.ap[:, :], ROUND, ROUND, ALU.add, ALU.subtract), *(out_work.take() if i == 0 else []))
                    s.free, o.free = [], []
                return step

            def turn_quant():
                w, bk = out_work, bank_for()
                pb, q = bk.ap[:, :].bitcast(BF16), w.ap[:, S:2 * S].bitcast(BF16)
                PE.wait(V.last)
                for n in range(ST * DC):
                    f = lambda e, n=n: e.transpose(pb[:, n * P:(n + 1) * P], q[:, n * P:(n + 1) * P], identb[:, :])
                    done = PE.do(f) if n == ST * DC - 1 else PE.quiet(f)
                st["qT"] = V.do(lambda e: e.tensor_copy(w.ap[:, 0:S].bitcast(BF16), pb), done)
                bk.free = [st["qT"]]

            def linear(h):
                def step():
                    w, bk = out_work, bank_for()
                    qT = w.ap[:, 0:S].bitcast(BF16)
                    PE.wait(st["qT"])
                    for n in range(2):
                        i = 2 * h + n
                        for c in range(DC):
                            f = lambda e, i=i, n=n, c=c: e.matmul(bk.ap[:, n * D:(n + 1) * D], qT[:, (i * DC + c) * P:(i * DC + c + 1) * P],
                                                                  tern_w[:, c, :], start=c == 0, stop=c == DC - 1)
                            done = PE.do(f) if n and c == DC - 1 else PE.quiet(f)
                    if h == 1:
                        w.free = [done]
                    for n in range(2):
                        xi = x.ap[:, 2 * h + n, :]
                        V.do(lambda e, xi=xi: e.tensor_tensor(xi, xi, lin_bias[:, :], ALU.add))
                        V.then(lambda e, xi=xi, n=n: e.scalar_tensor_tensor(out=xi, in0=bk.ap[:, n * D:(n + 1) * D], scalar=gated_step,
                                                                            in1=xi, op0=ALU.mult, op1=ALU.add), done)
                    bk.free = [V.last]
                    if h == 1:
                        slot = xs[b]
                        slot.free = [SP.dma(lambda e: e.dma_start(a["out"][b].rearrange("(i p) d -> p i d", p=P), slot.ap[:, :, :]),
                                            slot.gate, V.last)]
                return step

            return ([scores, turn, softmax, weigh, weigh_with("ws", mulw), weigh_with("bs", addw), squash, apply, apply_to_x]
                    + norm_stats("lin", x, stats4)) + [quantize(i) for i in range(ST)] + [turn_quant, linear(0), linear(1)]

        unfinished = []

        def mix(gi):
            g = GROUPS[gi]
            steps = mix_in(g[0]) + [feature(g[0], 0), feature(g[0], 1)]
            for n, b in enumerate(g):
                out = unfinished[:]
                steps += out[:1] + merge(tanh_steps(b, 0), out[1:])
                a1 = tanh_steps(b, 1)
                flush = a1.pop()
                more = []
                if n + 1 < len(g):
                    a1 = merge(a1, mix_in(g[n + 1]) + [feature(g[n + 1], 0)])
                    more = [feature(g[n + 1], 1)]
                steps += a1 + [flush] + more
                unfinished[:] = mix_out(b)
            return steps

        late_prologue()
        temps_read = [PE.last, V.last]
        experts_in = [None]

        def load_weights():
            load_expert(shared_w[:, :], a["WgsT"], a["WusT"], a["WdsT"])
            zero_rows(rows_dram[0])
            for k in range(E):
                load_expert(expert_w[:, k, :], a["WgT"][k], a["WuT"][k], a["WdT"][k], *(temps_read if k >= E - 2 else []))
            zero_rows(rows_dram[1])
            experts_in[0] = g_exp.token()

        def run(steps):
            for s in steps:
                s()

        def attends(gi):
            return [s for b in GROUPS[gi] for s in attend(b)] + route(gi)

        NG = len(GROUPS)
        first = attends(0)
        run(first[:1])
        load_weights()
        run(first[1:])
        misc.slots, misc.at = [banks[7]], 0
        for gi in range(NG):
            tile_steps = expert_steps(gi)
            run(tile_steps[:4])
            beside = [tile_steps[4:]]
            if gi + 1 < NG:
                beside.append(attends(gi + 1))
            if gi:
                beside.append(mix(gi - 1))
            run(merge(*beside))
        misc.slots = [banks[i] for i in (7, 0, 1, 2, 3, 4, 5)]
        on_scalar_too[0] = False
        run(mix(NG - 1) + unfinished)
        SP.wait(*[t for x in stream.slots for t in x.free])

        block = ctx.enter_context(nc.Block())
        for name, lane in (("sync", SP), ("gpsimd", G), ("scalar", A), ("vector", V), ("tensor", PE)):
            def body(e, lane=lane):
                for op in lane.ops:
                    op(e)
            {"sync": block.sync, "gpsimd": block.gpsimd, "scalar": block.scalar, "vector": block.vector,
             "tensor": block.tensor}[name](body)


class _Later:

    def __init__(self, xs, b):
        self.xs, self.b = xs, b

    @property
    def ap(self):
        return self.xs[self.b].ap

    def __getitem__(self, key):
        return self.xs[self.b].ap[key]


def kernel(**inputs):
    import numpy as np
    import concourse.bacc as bacc
    from concourse.bass_utils import run_bass_kernel_spmd

    i = {k: np.asarray(v) for k, v in inputs.items()}
    B, T = i["ctx_1024"].shape[0], i["ctx_1024"].shape[1]
    D = i["x"].shape[2]
    vectors = ("L0_xattn_bk", "L1_xattn_b", "L1_xattn_w", "L1_xattn_Wcw", "L1_xattn_Wcb", "L0_xattn_bq")
    cols = np.concatenate([i[n].reshape(D // P, P).T for n in vectors], axis=1)
    numbers = ("g_xattn", "g_ffn", "L0_xattn_beta_risk", "L0_xattn_beta_prio", "L0_xattn_beta_impl",
               "L1_ffn_act_scale", "L1_xattn_bcw", "L1_xattn_bcb")
    scalars = np.concatenate([i[n].reshape(1, -1) for n in numbers], axis=1)
    arrays = {
        "x": i["x"], "fside": i["fside_BxSxS2_0"],
        "ctxT": i["ctx_1024"].reshape(B * T, D).T,
        "mask": i["mask_BxS2_ik0"].reshape(1, B * T),
        "Wq": i["L0_xattn_Wq"], "WkT": i["L0_xattn_Wk"].T, "WvT": i["L0_xattn_Wv"].T,
        "bv": i["L0_xattn_bv"].reshape(1, D), "cols": cols, "scalars": scalars,
        "WgsT": i["L0_ffn_Wg_s"].T, "WusT": i["L0_ffn_Wu_s"].T, "WdsT": i["L0_ffn_Wd_s"].T,
        "WgT": i["L0_ffn_Wg"].transpose(0, 2, 1), "WuT": i["L0_ffn_Wu"].transpose(0, 2, 1),
        "WdT": i["L0_ffn_Wd"].transpose(0, 2, 1),
        "WrT": i["L0_ffn_Wr"].T, "rb": i["L0_ffn_rb"].reshape(1, -1),
        "Ws": i["L1_xattn_Ws"], "W": i["L1_xattn_W"],
        "ternT": i["L1_ffn_ternary_weight"].T, "lin_bias": i["L1_ffn_bias"].reshape(1, D),
    }
    nc = bacc.Bacc("TRN2", target_bir_lowering=False, num_devices=1, dynamic_dma_scratch_size=4096)
    feed, args = {}, {}
    for name, v in arrays.items():
        v = np.ascontiguousarray(v)
        feed[f"in_{name}"] = v
        args[name] = nc.dram_tensor(f"in_{name}", v.shape, mybir.dt.from_np(v.dtype), kind="ExternalInput").ap()
    args["out"] = nc.dram_tensor("out", i["x"].shape, F32, kind="ExternalOutput").ap()
    build(nc, args)
    r = run_bass_kernel_spmd(nc, [feed], core_ids=[0])
    return r.results[0]["out"]
```

```python
from contextlib import ExitStack

import concourse.bass as bass
from concourse import mybir

F32 = mybir.dt.float32
BF16 = mybir.dt.bfloat16
I32 = mybir.dt.int32
U32 = mybir.dt.uint32
ALU = mybir.AluOpType
ACT = mybir.ActivationFunctionType
AX = mybir.AxisListType.X

P = 128
LN_EPS = 1e-5
NEG = -1e30
MIN_SCALE = 1e-5
QMAX = 127.0
ROUND = 1.5 * 2 ** 23
FLT_MAX = 3.4028234e38

GROUPS = [[0], [1, 2], [3, 4], [5, 6], [7]]


class Lane:

    def __init__(self, sem):
        self.sem, self.count, self.ops, self.seen, self.last = sem, 0, [], {}, None

    def wait(self, *tokens):
        for sem, value in tokens:
            if self.seen.get(sem.name, 0) < value:
                self.seen[sem.name] = value
                self.ops.append(lambda e, s=sem, v=value: e.wait_ge(s, v))

    def do(self, instruction, *after):
        self.wait(*after)
        self.count += 1
        self.ops.append(lambda e: instruction(e).then_inc(self.sem, 1))
        self.last = (self.sem, self.count)
        return self.last

    def then(self, instruction, *after):
        return self.do(instruction, self.last, *after)

    def quiet(self, instruction):
        self.ops.append(instruction)

    def dma(self, transfer, gate, *after):
        self.wait(*after)
        gate.count += 16
        self.ops.append(lambda e: transfer(e).then_inc(gate.sem, 16))
        return (gate.sem, gate.count)


class Gate:

    def __init__(self, sem):
        self.sem, self.count = sem, 0

    def token(self):
        return (self.sem, self.count)


class Slot:

    def __init__(self, ap, gate=None, pool_gate=None):
        self.ap, self.gate, self.pool_gate, self.free, self.ready = ap, gate, pool_gate, [], None

    def take(self):
        assert self.free is not None, "taken before its last user gave it back"
        tokens, self.free = self.free, None
        return tokens


class Ring:
    def __init__(self, slots):
        self.slots, self.at = slots, -1

    def next(self):
        for _ in self.slots:
            self.at += 1
            slot = self.slots[self.at % len(self.slots)]
            if slot.free is not None:
                return slot
        assert False, "all slots are held"


def merge(*lists):
    keyed = [((i + 0.5) / len(l), n, i, s) for n, l in enumerate(lists) for i, s in enumerate(l)]
    return [s for _, _, _, s in sorted(keyed, key=lambda k: k[:3])]


def pause():
    pass


def build(nc, a):
    B, S, D = a["x"].shape
    T = a["fside"].shape[2]
    E, _, I = a["WgT"].shape
    DC, IC, ST = D // P, I // P, S // P
    BT = B * T
    SCALE = float(D) ** -0.5
    EW = 2 * DC * I + IC * D
    GT = [len(g) * ST for g in GROUPS]
    RT = [2 * n + E - 1 for n in GT]
    NTM, RTM, NG = max(GT), max(RT), len(GROUPS)
    assert sum(GROUPS, []) == list(range(B)) and D == 2 * P and T == 64 and S == 512 and I == 512

    ctx = ExitStack()
    with ctx:
        def sb(name, shape, dt=F32):
            return ctx.enter_context(nc.sbuf_tensor(name, shape, dt))

        def sem(name):
            return ctx.enter_context(nc.semaphore(name))

        def gate(name):
            return Gate(sem(name))

        expert_w = sb("expert_w", [P, E, EW])
        shared_w = sb("shared_w", [P, EW])
        stream = Ring([Slot(sb(f"x{i}", [P, ST, D]), gate(f"s_x{i}")) for i in range(6)])
        normT = Slot(sb("normT", [P, DC * S]))
        featT = [Slot(sb(f"featT{c}", [P, S])) for c in range(DC)]
        normed = Ring([Slot(sb(f"normed{i}", [P, D]), gate(f"s_normed{i}"), gate(f"s_scatter{i}")) for i in range(6)])
        wide = Ring([Slot(sb(f"wide{i}", [P, 1024])) for i in range(4)])
        attn_work, out_work = Slot(sb("attn_work", [P, 1024])), Slot(sb("out_work", [P, 1024]))
        act = Ring([Slot(sb(f"act{i}", [P, I])) for i in range(2)])
        actT = Slot(sb("actT", [P, I]))
        rowsT = Ring([Slot(sb(f"rowsT{i}", [P, D])) for i in range(2)])
        rows_out = Ring([Slot(sb(f"rows_out{i}", [P, D]), gate(f"s_rows_out{i}")) for i in range(2)])
        picked = Ring([Slot(sb(f"picked{i}", [P, D]), gate(f"s_picked{i}")) for i in range(3)])
        score = Slot(sb("score", [P, ST, T]), gate("s_score"))
        rho = sb("rho", [P, ST, T])
        rho_e = sb("rho_e", [P, ST, T])

        txtT = sb("txtT", [P, DC, BT])
        keysq = sb("keysq", [P, DC, BT])
        values = sb("values", [P, B // 2, D])
        feat_w = sb("feat_w", [P, DC, D])
        router_w = sb("router_w", [P, DC, E])
        tern_w = sb("tern_w", [P, DC, D], BF16)
        maskadd = sb("maskadd", [P, BT])
        mulw = sb("mulw", [P, BT])
        addw = sb("addw", [P, BT])
        lin_bias = sb("lin_bias", [P, D])
        pick_w = sb("pick_w", [P, DC, 63])
        row_qb = sb("row_qb", [1, BT])
        row_bv = sb("row_bv", [1, D])
        row_rb = sb("row_rb", [1, E])
        ident = sb("ident", [P, P])
        identb = sb("identb", [P, P], BF16)
        before = sb("before", [P, P])
        ones = sb("ones", [P, P])
        rank8 = sb("rank8", [P, E])
        below = sb("below", [P, E, E])
        steps128 = sb("steps128", [P, NTM])
        tile_id = sb("tile_id", [P, RTM])
        halves = sb("halves", [P, ST])
        cols = sb("cols", [P, 6 * DC])
        scal = sb("scal", [P, 16])
        ln = {k: dict(stats=sb(f"ln_{k}_stats", [P, ST, 6]), mv=sb(f"ln_{k}_mv", [P, NTM, 2]),
                      var=sb(f"ln_{k}_var", [P, ST]), r=sb(f"ln_{k}_r", [P, NTM]),
                      t=sb(f"ln_{k}_t", [P, ST])) for k in ("att", "moe0", "moe1", "mix0", "mix1", "lin")}
        sm = {k: sb(f"sm_{k}", [P, ST]) for k in ("amax", "asum", "rmax", "rsum", "ws", "bs", "A", "B", "t")}
        prob = sb("prob", [P, NTM, E])
        prob2 = sb("prob2", [P, NTM, E])
        hot = [sb(f"hot{k}", [P, NTM, E]) for k in range(2)]
        chosen = sb("chosen", [P, NTM + 1, E])
        posn = sb("posn", [P, NTM + 1, E])
        rt = sb("rt", [P, NTM, E])
        rt2 = sb("rt2", [P, E, E])
        rs = {k: sb(f"rs_{k}", [P, n]) for k, n in
              dict(best=NTM, tiles=E, base=E, pos=NTM, cum=E, eid=RTM).items()}
        cmp_id = sb("cmp_id", [P, RTM, E])
        slot_of = [[sb(f"slot_of{g}{k}", [P, NTM], U32) for k in range(2)] for g in range(2)]
        share = [[sb(f"share{g}{k}", [P, NTM]) for k in range(2)] for g in range(2)]
        owner = [sb(f"owner{g}", [P, RTM], I32) for g in range(2)]

        banks = [Slot(ctx.enter_context(nc.psum_tensor(f"bank{i}", [P, 512], F32))) for i in range(8)]
        up_banks = [(banks[0], banks[1]), (banks[2], banks[3])]
        actT_bank, row_bank, rho_bank = banks[4], banks[5], banks[6]
        misc = Ring([banks[7], banks[0], banks[1], banks[2], banks[3], banks[4], banks[5]])

        rows_dram = [nc.dram_tensor(f"rows_by_expert{g}", (RTM * P, D), F32, kind="Internal").ap() for g in range(2)]
        norm_dram = nc.dram_tensor("norm_rows", (NTM, P, D), F32, kind="Internal").ap()
        outs_dram = [nc.dram_tensor(f"expert_rows{g}", (RTM * P, D), F32, kind="Internal").ap() for g in range(2)]

        V, A, PE, G, SP = (Lane(sem(n)) for n in ("s_vector", "s_scalar", "s_tensor", "s_gpsimd", "s_sync"))

        tail = expert_w[:, E - 2:E, :].rearrange("p e n -> p (e n)")
        at = [0]

        def temp(n, dt=F32):
            v = tail[:, at[0]:at[0] + n]
            at[0] += n
            return v.bitcast(dt) if dt is not F32 else v

        ctxT = temp(DC * BT).rearrange("p (c n) -> p c n", c=DC)
        wk, wv, wq, ws = (temp(DC * D).rearrange("p (c n) -> p c n", c=DC) for _ in range(4))
        keysT = temp(DC * BT).rearrange("p (c n) -> p c n", c=DC)
        spread_w = temp(2 * DC * P).rearrange("p (k n) -> p k n", n=P)
        mask_i = temp(BT, I32)
        tern_i = temp(DC * D, I32).rearrange("p (c n) -> p c n", c=DC)
        assert at[0] <= 2 * EW

        def chunked(ap):
            return ap.rearrange("(c p) n -> p c n", p=P)

        g_ctx, g_wts, g_small, g_late = gate("s_ctx"), gate("s_proj_w"), gate("s_small"), gate("s_late")
        for dst, src in ((ctxT, chunked(a["ctxT"])), (wk, chunked(a["WkT"]))):
            SP.dma(lambda e, d=dst, s=src: e.dma_start(d, s), g_ctx)
        BK, TB, WW, CW, CB, BQ = (k * DC for k in range(6))
        GX, GF, BR, ASC, BCW, BCB = 0, 2, 4, 7, 8, 9
        for dst, src in ((cols[:, :], a["cols"]), (row_bv[:, :], a["bv"]), (row_rb[:, :], a["rb"]),
                         (scal[:, 0:10], a["scalars"].to_broadcast([P, 10]))):
            SP.dma(lambda e, d=dst, s=src: e.dma_start(d, s), g_small)
        for dst, src in ((wq, chunked(a["Wq"])), (wv, chunked(a["WvT"])), (ws, chunked(a["Ws"]))):
            SP.dma(lambda e, d=dst, s=src: e.dma_start(d, s), g_wts)
        small_in = g_small.token()

        for m in (ident, identb):
            c = G.do(lambda e, m=m: e.memset(m[:, :], 0.0))
            G.do(lambda e, m=m: e.affine_select(out=m[:, :], in_=m[:, :], compare_op=ALU.not_equal, fill=1.0, base=0,
                                                pattern=[[-1, P]], channel_multiplier=1), c)
        ident_ok = G.last
        c = G.do(lambda e: e.memset(before[:, :], 1.0))
        G.do(lambda e: e.affine_select(out=before[:, :], in_=before[:, :], compare_op=ALU.is_gt, fill=0.0, base=0,
                                       pattern=[[1, P]], channel_multiplier=-1), c)
        G.do(lambda e: e.memset(ones[:, :], 1.0))
        ones_ok = G.last
        G.do(lambda e: e.memset(halves[:, :], -0.5))
        for ap, pattern, base in ((rank8[:, :], [[-1, E]], E), (below[:, :, :], [[1, E], [-1, E]], 0),
                                  (steps128[:, :], [[P, NTM]], 0), (tile_id[:, :], [[1, RTM]], 0)):
            G.do(lambda e, o=ap, p=pattern, b=base: e.iota(o, pattern=p, base=b, channel_multiplier=0,
                                                           allow_small_or_imprecise_dtypes=True))
        consts_ok = G.last
        V.do(lambda e: e.tensor_scalar(below[:, :, :], below[:, :, :], 0.0, None, ALU.is_gt), consts_ok)

        zeros = picked.slots[-1]
        zero_ok = V.do(lambda e: e.memset(zeros.ap[:, :], 0.0))
        g_zero = gate("s_zero")

        def zero_rows(r):
            src = zeros.ap[:, :].unsqueeze(1).to_broadcast([P, RTM, D])
            SP.dma(lambda e: e.dma_start(r.rearrange("(n p) d -> p n d", p=P), src), g_zero, zero_ok)
            zeros.free = [g_zero.token()]

        gates_ok = A.do(lambda e: e.activation(scal[:, GX:GX + 4], scal[:, GX:GX + 4], ACT.Tanh), small_in)
        V.wait(gates_ok)
        GX0, GX1, GF0, GF1 = (scal[:, k:k + 1] for k in (GX, GX + 1, GF, GF + 1))
        V.do(lambda e: e.tensor_tensor(scal[:, BR:BR + 1], scal[:, BR:BR + 1], scal[:, BR + 1:BR + 2], ALU.add))
        V.then(lambda e: e.tensor_tensor(scal[:, BR:BR + 1], scal[:, BR:BR + 1], scal[:, BR + 2:BR + 3], ALU.subtract))
        side_w = scal[:, BR:BR + 1]
        V.do(lambda e: e.tensor_scalar(scal[:, ASC:ASC + 1], scal[:, ASC:ASC + 1], MIN_SCALE, FLT_MAX, ALU.max, ALU.min))
        V.then(lambda e: e.reciprocal(scal[:, 10:11], scal[:, ASC:ASC + 1]))
        V.do(lambda e: e.tensor_tensor(scal[:, 11:12], scal[:, ASC:ASC + 1], GF1, ALU.mult))
        inv_step, gated_step = scal[:, 10:11], scal[:, 11:12]
        c = V.do(lambda e: e.memset(pick_w[:, :, :], 0.0))
        for k in range(DC):
            V.do(lambda e, k=k: e.tensor_copy(pick_w[:, k, 31:32], cols[:, WW + k:WW + k + 1]), c)
        for k in range(2 * DC):
            V.do(lambda e, k=k: e.tensor_copy(spread_w[:, k, :], cols[:, CW + k:CW + k + 1].to_broadcast([P, P])))
        prep_ok = V.last

        def bank_for(pe=PE):
            b = misc.next()
            PE.wait(*b.take())
            return b

        def project(out, lhs, rhs, n, bias=None, row=None, parts=P):
            b = bank_for()
            for c in range(DC):
                stop = c == DC - 1 and row is None
                f = lambda e, c=c, stop=stop: e.matmul(b.ap[0:parts, 0:n], lhs(c), rhs(c), start=c == 0, stop=stop)
                done = PE.do(f) if stop else PE.quiet(f)
            if row is not None:
                done = PE.do(lambda e: e.matmul(b.ap[0:parts, 0:n], ones[0:1, 0:parts], row, start=False, stop=True))
            if bias is None:
                b.free = [A.do(lambda e: e.activation(out, b.ap[0:parts, 0:n], ACT.Copy), done)]
            else:
                b.free = [V.do(lambda e: e.tensor_scalar(out, b.ap[0:parts, 0:n], bias, None, ALU.add), done)]

        PE.wait(g_ctx.token(), small_in, ident_ok, ones_ok, prep_ok)
        for o in range(DC):
            project(keysT[:, o, :], lambda c, o=o: wk[:, c, o * P:(o + 1) * P], lambda c: ctxT[:, c, :], BT,
                    bias=cols[:, BK + o:BK + o + 1])
        PE.wait(V.last, g_wts.token())
        for o in range(DC):
            project(keysq[:, o, :], lambda c, o=o: wq[:, c, o * P:(o + 1) * P], lambda c: keysT[:, c, :], BT)
        project(row_qb[0:1, :], lambda c: cols[:, BQ + c:BQ + c + 1], lambda c: keysT[:, c, :], BT, parts=1)
        for j in range(B // 2):
            project(values[:, j, :], lambda c, j=j: ctxT[:, c, 2 * T * j:2 * T * (j + 1)], lambda c: wv[:, c, :], D,
                    row=row_bv[0:1, :])
        attn_ready = [A.last]

        def late_prologue():
            def load():
                for dst, src in ((router_w[:, :, :], chunked(a["WrT"])), (feat_w[:, :, :], chunked(a["W"])),
                                 (tern_i, chunked(a["ternT"])), (lin_bias[:, :], a["lin_bias"].to_broadcast([P, D])),
                                 (mask_i, a["mask"].to_broadcast([P, BT]))):
                    SP.dma(lambda e, d=dst, s=src: e.dma_start(d, s), g_late)

            def text(o):
                project(txtT[:, o, :], lambda c: ws[:, c, o * P:(o + 1) * P], lambda c: ctxT[:, c, :], BT,
                        bias=cols[:, TB + o:TB + o + 1])

            def spread():
                project(mulw[:, :], lambda c: spread_w[:, c, :], lambda c: ctxT[:, c, :], BT)
                project(addw[:, :], lambda c: spread_w[:, DC + c, :], lambda c: ctxT[:, c, :], BT)

            def convert():
                V.do(lambda e: e.tensor_scalar(tern_w[:, :, :], tern_i, 1.0, None, ALU.subtract), g_late.token())
                V.do(lambda e: e.tensor_scalar(maskadd[:, :], mask_i, -1.0, 1.0, ALU.mult, ALU.add))
                V.then(lambda e: e.tensor_scalar(maskadd[:, :], maskadd[:, :], NEG, None, ALU.mult))
                V.do(lambda e: e.tensor_scalar(lin_bias[:, :], lin_bias[:, :], GF1, None, ALU.mult))
                PE.wait(g_late.token())
            return [load, lambda: text(0), lambda: text(1), spread, convert]

        g_exp = gate("s_experts")

        g_shared = gate("s_shared")

        def load_expert(gate, dst, WgT, WuT, WdT, *after):
            n = DC * I
            for lo, src, rows in ((0, WgT, n), (n, WuT, n), (2 * n, WdT, IC * D)):
                inner = I if src is not WdT else D
                SP.dma(lambda e, lo=lo, s=src, r=rows, i=inner: e.dma_start(
                    dst[:, lo:lo + r].rearrange("p (c n) -> p c n", n=i), chunked(s)), gate, *after)

        def norm_stats(k, x, ok, first=0):
            s, st = ln[k], {}
            var, r, t = s["var"][:, :], s["r"][:, first:first + ST], s["t"][:, :]

            def stats():
                for i in range(ST):
                    V.do(lambda e, i=i: e.bn_stats(s["stats"][:, i, :], x[:, i, :]))

            def aggregate():
                V.wait(V.last)
                for i in range(ST):
                    V.do(lambda e, i=i: e.bn_aggr(s["mv"][:, first + i, :], s["stats"][:, i, :]))

            def power():
                c = V.then(lambda e: e.tensor_scalar(var, s["mv"][:, first:first + ST, 1], LN_EPS, None, ALU.add))
                st["r"] = G.do(lambda e: e.tensor_tensor(r, var, halves[:, :], ALU.pow), c)

            def newton():
                V.do(lambda e: e.tensor_tensor(t, r, r, ALU.mult), st["r"])
                V.then(lambda e: e.tensor_tensor(t, t, var, ALU.mult))
                V.then(lambda e: e.tensor_scalar(t, t, -0.5, 1.5, ALU.mult, ALU.add))
                ok[0] = V.then(lambda e: e.tensor_tensor(r, r, t, ALU.mult))
            return [stats, aggregate, power, newton]

        def normalize(k, x, i, at, stats_ok):
            s, slot = ln[k], normed.next()
            slot.ready = V.do(lambda e: e.tensor_scalar(slot.ap[:, :], x[:, i, :], s["mv"][:, at, 0:1], s["r"][:, at:at + 1],
                                                        ALU.subtract, ALU.mult), stats_ok, *slot.take())
            slot.free = [slot.ready]
            return slot

        def chunks(slot):
            return slot.ap[:, :].rearrange("p (c n) -> p c n", c=DC)

        def transpose_norm(k, x, first, stats_ok, box, target, keep=None):
            slots = []

            def scale(h):
                for i in (2 * h, 2 * h + 1):
                    slot = normalize(k, x, i, first + i, stats_ok[0])
                    slot.free = None
                    slots.append(slot)

            def turn(h):
                b = bank_for()
                for n in range(2):
                    slot = slots.pop(0)
                    PE.wait(slot.ready)
                    for c in range(DC):
                        f = lambda e, n=n, c=c, s=slot: e.transpose(b.ap[:, (n * DC + c) * P:(n * DC + c + 1) * P],
                                                                    s.ap[:, c * P:(c + 1) * P], ident[:, :])
                        done = PE.do(f) if c == DC - 1 else PE.quiet(f)
                    slot.free = [done] + ([keep(2 * h + n, slot)] if keep else [])
                out = chunks(target).rearrange("p c (i n) -> p i c n", n=P)[:, 2 * h:2 * h + 2, :, :]
                b.free = [V.do(lambda e: e.tensor_copy(out, b.ap[:, :].rearrange("p (i c n) -> p i c n", i=2, c=DC)),
                               done, *(target.take() if h == 0 else []))]
                box[:] = [V.last]

            def both():
                turn(0)
                scale(1)
            return [lambda: scale(0), both, lambda: turn(1)]

        ATTENTION = 23
        xs = {}
        normT_ok = {}
        kept, norm_read = {}, {}

        def attend(b):
            st = {}
            gi = next(i for i, g in enumerate(GROUPS) if b in g)
            first = GROUPS[gi].index(b) * ST
            key = f"moe{gi % 2}"
            half = (b % 2) * T
            stats1, stats2, lnT1, lnT2 = [None], [None], [], []

            def load():
                x = xs[b] = stream.next()
                x.ready = SP.dma(lambda e: e.dma_start(x.ap[:, :, :], a["x"][b].rearrange("(i p) d -> p i d", p=P)),
                                 x.gate, *x.take())

            def load_side():
                st["side"] = SP.dma(lambda e: e.dma_start(score.ap[:, :, :], a["fside"][b].rearrange("(i p) d -> p i d", p=P)),
                                    score.gate, *score.take())

            def arrived():
                V.wait(xs[b].ready)
                V.do(lambda e: e.tensor_scalar(score.ap[:, :, :], score.ap[:, :, :], side_w, None, ALU.mult), st["side"])

            def scores():
                bk = bank_for()
                PE.wait(*lnT1, *attn_ready)
                PE.quiet(lambda e: e.matmul(bk.ap[:, 0:ST * T].rearrange("p (i t) -> p i t", t=T), ones[0:1, :],
                                            row_qb[0:1, b * T:(b + 1) * T].unsqueeze(1).to_broadcast([1, ST, T]), start=True, stop=False))
                for i in range(ST):
                    for c in range(DC):
                        f = lambda e, c=c, i=i: e.matmul(bk.ap[:, i * T:(i + 1) * T], attn_work.ap[:, c * S + i * P:c * S + (i + 1) * P],
                                                         keysq[:, c, b * T:(b + 1) * T], start=False, stop=(i, c) == (ST - 1, DC - 1))
                        done = PE.do(f) if c == DC - 1 and i == ST - 1 else PE.quiet(f)
                st["scored"] = done
                sc = score.ap
                bk.free = [V.do(lambda e: e.scalar_tensor_tensor(out=sc[:, :, :], in0=bk.ap[:, 0:ST * T].rearrange("p (i t) -> p i t", t=T),
                                                                 scalar=SCALE, in1=sc[:, :, :], op0=ALU.mult, op1=ALU.add), V.last, done)]

            def softmax():
                sc, m = score.ap, sm["amax"]
                V.then(lambda e: e.tensor_reduce(m[:, :], sc[:, :, :], AX, ALU.max))
                V.then(lambda e: e.tensor_tensor(sc[:, :, :], sc[:, :, :], m[:, :].unsqueeze(2).to_broadcast([P, ST, T]), ALU.subtract))
                w = st["w"] = attn_work
                ex = st["ex"] = w.ap[:, 0:ST * P].rearrange("p (i t) -> p i t", t=P)[:, :, half:half + T]
                st["e"] = A.do(lambda e: e.activation(ex, sc[:, :, :], ACT.Exp), V.last, st["scored"])
                score.free = [st["e"]]

            def sums():
                V.do(lambda e: e.tensor_reduce(sm["asum"][:, :], st["ex"], AX, ALU.add), st["e"])
                V.then(lambda e: e.reciprocal(sm["asum"][:, :], sm["asum"][:, :]))
                st["sum"] = V.then(lambda e: e.tensor_scalar(sm["asum"][:, :], sm["asum"][:, :], GX0, None, ALU.mult))

            def turn():
                bk, w = bank_for(), st["w"]
                PE.wait(st["e"])
                for i in range(ST):
                    f = lambda e, i=i: e.transpose(bk.ap[:, i * P:(i + 1) * P], w.ap[:, i * P:(i + 1) * P], ident[:, :])
                    done = PE.do(f) if i == ST - 1 else PE.quiet(f)
                st["eT"] = A.do(lambda e: e.activation(w.ap[:, 512:1024], bk.ap[:, :], ACT.Copy), done)
                bk.free = [st["eT"]]

            def weigh(h):
                def step():
                    bk, w, x = bank_for(), st["w"], xs[b].ap
                    PE.wait(st["eT"])
                    for n in range(2):
                        i = 2 * h + n
                        f = lambda e, i=i, n=n: e.matmul(bk.ap[:, n * D:(n + 1) * D], w.ap[half:half + T, 512 + i * P:512 + (i + 1) * P],
                                                         values[half:half + T, b // 2, :], start=True, stop=True)
                        done = PE.do(f) if n else PE.quiet(f)
                    if h == 1:
                        w.free = [done]
                    for n in range(2):
                        i = 2 * h + n
                        V.do(lambda e, i=i, n=n: e.scalar_tensor_tensor(
                            out=x[:, i, :], in0=bk.ap[:, n * D:(n + 1) * D], scalar=sm["asum"][:, i:i + 1], in1=x[:, i, :],
                            op0=ALU.mult, op1=ALU.add), done, st["sum"])
                    bk.free = [V.last]
                return step

            def attended():
                V.wait(V.last)

            def keep(i, slot):
                tok = G.dma(lambda e: e.dma_start(norm_dram[first + i], slot.ap[:, :]), slot.pool_gate, slot.ready,
                             *norm_read.get(first + i, []))
                kept[first + i] = tok
                return tok

            def logits():
                bk = bank_for()
                normT_ok[b] = lnT2
                PE.wait(*lnT2)
                PE.quiet(lambda e: e.matmul(bk.ap[:, 0:ST * E].rearrange("p (i n) -> p i n", n=E), ones[0:1, :],
                                            row_rb[0:1, :].unsqueeze(1).to_broadcast([1, ST, E]), start=True, stop=False))
                for i in range(ST):
                    for c in range(DC):
                        f = lambda e, c=c, i=i: e.matmul(bk.ap[:, i * E:(i + 1) * E], normT.ap[:, c * S + i * P:c * S + (i + 1) * P],
                                                         router_w[:, c, :], start=False, stop=(i, c) == (ST - 1, DC - 1))
                        done = PE.do(f) if c == DC - 1 and i == ST - 1 else PE.quiet(f)
                pr = prob[:, first:first + ST, :]
                bk.free = [A.do(lambda e: e.activation(pr, bk.ap[:, 0:ST * E].rearrange("p (i n) -> p i n", n=E), ACT.Exp, scale=-1.0),
                                done, *prob_free)]
                st["p"] = A.last

            def sigmoid():
                pr = prob[:, first:first + ST, :]
                V.do(lambda e: e.tensor_scalar(pr, pr, 1.0, None, ALU.add), st["p"])
                V.then(lambda e: e.reciprocal(pr, pr))

            x = _Later(xs, b)
            return ([load, load_side, pause, pause, arrived] + norm_stats("att", x, stats1) + transpose_norm("att", x, 0, stats1, lnT1, attn_work)
                    + [scores, softmax, sums, turn, weigh(0), weigh(1), attended] + norm_stats(key, x, stats2, first)
                    + transpose_norm(key, x, first, stats2, lnT2, normT, keep) + [logits, sigmoid])

        prob_free = []

        def route(gi):
            par, n, R, group = gi % 2, GT[gi], RT[gi], GROUPS[gi]
            pr, p2, ch, rb = prob[:, 0:n, :], prob2[:, 0:n, :], chosen[:, 0:n, :], rt[:, 0:n, :]
            best = rs["best"][:, 0:n]

            def wide_(v):
                return v.unsqueeze(2).to_broadcast([P, n, E])

            def choose(k):
                rank = rank8[:, :].unsqueeze(1).to_broadcast([P, n, E])

                def step():
                    src, top, h = (pr, p2)[k], share[par][k][:, 0:n], hot[k][:, 0:n, :]
                    V.then(lambda e, s=src, t=top: e.tensor_reduce(t, s, AX, ALU.max))
                    V.then(lambda e, s=src, t=top: e.tensor_tensor(rb, s, wide_(t), ALU.is_equal))
                    V.then(lambda e: e.tensor_tensor(rb, rb, rank, ALU.mult))
                    V.then(lambda e: e.tensor_reduce(best, rb, AX, ALU.max))
                    V.then(lambda e, h=h: e.tensor_tensor(h, rank, wide_(best), ALU.is_equal))
                    if k == 0:
                        V.then(lambda e, h=h: e.scalar_tensor_tensor(out=p2, in0=h, scalar=-2.0, in1=pr, op0=ALU.mult, op1=ALU.add))
                return step

            def choice():
                prob_free[:] = [V.last]
                V.then(lambda e: e.tensor_tensor(ch, hot[0][:, 0:n, :], hot[1][:, 0:n, :], ALU.add))
                V.do(lambda e: e.memset(chosen[:, n, :], 0.0))
                for k in range(2):
                    V.do(lambda e, k=k: e.tensor_scalar(share[par][k][:, 0:n], share[par][k][:, 0:n], GF0, None, ALU.mult))

            def count():
                bk = bank_for()
                PE.wait(V.last, consts_ok)
                W = (n + 1) * E
                PE.quiet(lambda e: e.matmul(bk.ap[:, 0:W], before[:, :], chosen[:, 0:n + 1, :].rearrange("p i e -> p (i e)"), start=True, stop=False))
                for i in range(n):
                    m = n - i
                    f = lambda e, i=i, m=m: e.matmul(bk.ap[:, (i + 1) * E:W].rearrange("p (j e) -> p j e", e=E), ones[:, :],
                                                     chosen[:, i:i + 1, :].to_broadcast([P, m, E]), start=False, stop=i == n - 1)
                    done = PE.do(f) if i == n - 1 else PE.quiet(f)
                bk.free = [V.do(lambda e: e.tensor_copy(posn[:, 0:n + 1, :].rearrange("p i e -> p (i e)"), bk.ap[:, 0:W]), done)]

            def place():
                total = posn[:, n, :]
                t2 = rt2[:, :, :]
                tiles, base, cum = (rs[k][:, :] for k in ("tiles", "base", "cum"))
                V.then(lambda e: e.tensor_tensor(rt[:, 0:n, :].rearrange("p j e -> p e j"), total.unsqueeze(2).to_broadcast([P, E, n]),
                                                 steps128[:, 0:n].unsqueeze(1).to_broadcast([P, E, n]), ALU.is_gt))
                V.then(lambda e: e.tensor_reduce(tiles, rt[:, 0:n, :].rearrange("p j e -> p e j"), AX, ALU.add))
                V.then(lambda e: e.tensor_tensor(t2, below[:, :, :], tiles.unsqueeze(1).to_broadcast([P, E, E]), ALU.mult))
                V.then(lambda e: e.tensor_reduce(base, t2, AX, ALU.add))
                V.then(lambda e: e.tensor_tensor(cum, base, tiles, ALU.add))
                V.then(lambda e: e.tensor_scalar(base, base, float(P), None, ALU.mult))

            def place_rows():
                pos, base = posn[:, 0:n, :], rs["base"][:, :]
                V.then(lambda e: e.tensor_tensor(pos, pos, base.unsqueeze(1).to_broadcast([P, n, E]), ALU.add))
                for k in range(2):
                    V.then(lambda e, k=k: e.tensor_tensor(rb, hot[k][:, 0:n, :], pos, ALU.mult))
                    V.then(lambda e: e.tensor_reduce(rs["pos"][:, 0:n], rb, AX, ALU.add))
                    V.then(lambda e, k=k: e.tensor_copy(slot_of[par][k][:, 0:n], rs["pos"][:, 0:n]), *gathers_done[par])

            def place_owners():
                cum = rs["cum"][:, :]
                cm = cmp_id[:, 0:R, :]
                V.then(lambda e: e.tensor_tensor(cm, cum.unsqueeze(1).to_broadcast([P, R, E]),
                                                 tile_id[:, 0:R].unsqueeze(2).to_broadcast([P, R, E]), ALU.is_le))
                V.then(lambda e: e.tensor_reduce(rs["eid"][:, 0:R], cm, AX, ALU.add))
                placed[gi] = V.then(lambda e: e.tensor_scalar(owner[par][:, 0:R], rs["eid"][:, 0:R], float(E - 1), None, ALU.min),
                                    *owner_free[par])

            rows = {}

            def reload(i):
                def step():
                    slot = rows[i] = normed.next()
                    slot.ready = SP.dma(lambda e: e.dma_start(slot.ap[:, :], norm_dram[i]), slot.gate, kept[i], *slot.take())
                    norm_read[i] = [slot.ready]
                return step

            def scatter(i):
                def step():
                    slot = rows[i]
                    for k in range(2):
                        tok = G.dma(lambda e, k=k: e.indirect_dma_start(
                            out=rows_dram[par], out_offset=bass.IndirectOffsetOnAxis(ap=slot_of[par][k][:, i:i + 1], axis=0),
                            in_=slot.ap[:, :], in_offset=None), slot.pool_gate, slot.ready, placed[gi], *rows_free[par],
                            g_zero.token())
                    slot.free = [tok, slot.ready]
                    scattered.setdefault(gi, {})[slot.pool_gate.sem.name] = tok
                return step

            moves = [s for i in range(n + 2) for s in ([scatter(i - 2)] if i > 1 else []) + ([reload(i)] if i < n else [])]
            return [choose(0), choose(1), choice, pause, count, place, place_rows, place_owners] + moves

        placed, scattered = {}, {}
        gathers_done = [[], []]
        owner_free = [[], []]
        rows_free = [[], []]

        units = []
        work = {}
        stored = {}
        HALF = S // 2

        def shared_units(b):
            return [("shared", b, h, k) for h in range(2) for k in range(2)]

        def routed_units(gi):
            return [("routed", gi, s, None) for s in range(RT[gi])]

        def is_routed(n):
            return n < len(units) and units[n][0] == "routed"

        def fetch(n):
            if not is_routed(n) or "rows" in work.get(n, {}):
                return
            _, gi, s, _ = units[n]
            r = work.setdefault(n, {})["rows"] = normed.next()
            r.ready = SP.dma(lambda e: e.dma_start(r.ap[:, :], rows_dram[gi % 2][s * P:(s + 1) * P, :]), r.gate,
                             *r.take(), *scattered[gi].values())

        def turn_rows(n):
            if not is_routed(n) or "rowsT" in work.get(n, {}):
                return
            fetch(n)
            _, gi, s, _ = units[n]
            w = work[n]
            r = w["rows"]
            PE.wait(r.ready, *row_bank.take())
            for c in range(DC):
                f = lambda e, c=c: e.transpose(row_bank.ap[:, c * P:(c + 1) * P], r.ap[:, c * P:(c + 1) * P], ident[:, :])
                done = PE.do(f) if c == DC - 1 else PE.quiet(f)
            r.free = rows_free[gi % 2] = [done]
            t = w["lhsT"] = rowsT.next()
            w["rowsT"] = V.do(lambda e: e.tensor_copy(t.ap[:, :], row_bank.ap[:, 0:D]), done, *t.take())
            row_bank.free = [w["rowsT"]]

        N1 = DC * I

        def gate_products(n):
            kind, gi, s, _ = units[n]
            w = work.setdefault(n, {})
            w["banks"] = up_banks[n % 2]
            if kind == "routed":
                PE.wait(w["rowsT"], placed[gi], g_exp.token())

                def load_owner(e):
                    w["e"] = e.value_load(owner[gi % 2][0:1, s:s + 1], min_val=0, max_val=E - 1)
                PE.quiet(load_owner)
            else:
                PE.wait(*normT_ok[gi], g_shared.token())
            w["gate_ok"] = products(n, w["banks"][0], 0)

        def up_products(n):
            kind, b, h, k = units[n]
            w = work[n]
            w["up_ok"] = products(n, w["banks"][1], N1)
            if kind == "routed":
                w["lhsT"].free = [w["up_ok"]]
            elif (h, k) == (1, 1):
                normT.free = [w["up_ok"]]

        def expert_rows(w, lo, n):
            return expert_w[:, :, :].rearrange("p e n -> p (e n)")[:, bass.ds(w["e"] * EW + lo, n)]

        def products(n, bank, lo):
            kind, _, h, k = units[n]
            w = work[n]
            PE.wait(*bank.take())
            if kind == "routed":
                t = w["lhsT"].ap
                for c in range(DC):
                    f = lambda e, c=c: e.matmul(bank.ap[:, :], t[:, c * P:(c + 1) * P], expert_rows(w, lo + c * I, I),
                                                start=c == 0, stop=c == DC - 1)
                    done = PE.do(f) if c == DC - 1 else PE.quiet(f)
            else:
                for j in range(2):
                    for c in range(DC):
                        at = lo + c * I + (2 * k + j) * P
                        f = lambda e, c=c, j=j, at=at: e.matmul(bank.ap[:, j * HALF:(j + 1) * HALF], shared_w[:, at:at + P],
                                                                normT.ap[:, c * S + h * HALF:c * S + (h + 1) * HALF],
                                                                start=c == 0, stop=c == DC - 1)
                        done = PE.do(f) if (j, c) == (1, DC - 1) else PE.quiet(f)
            return done

        def gate_act(n):
            w = work[n]
            bg, bu = w["banks"]
            h = w["act"] = act.next()
            t = A.do(lambda e: e.activation(h.ap[:, :], bg.ap[:, :], ACT.Tanh, scale=0.5), w["gate_ok"], *h.take())
            V.do(lambda e: e.scalar_tensor_tensor(out=h.ap[:, :], in0=h.ap[:, :], scalar=1.0, in1=bg.ap[:, :],
                                                  op0=ALU.add, op1=ALU.mult), t)
            w["h"] = V.then(lambda e: e.scalar_tensor_tensor(out=h.ap[:, :], in0=h.ap[:, :], scalar=0.5, in1=bu.ap[:, :],
                                                             op0=ALU.mult, op1=ALU.mult), w["up_ok"])
            bg.free = bu.free = [w["h"]]

        def turn_act(n):
            if not is_routed(n):
                return
            w = work[n]
            h = w["act"]
            PE.wait(w["h"], *actT_bank.take())
            for c in range(IC):
                f = lambda e, c=c: e.transpose(actT_bank.ap[:, c * P:(c + 1) * P], h.ap[:, c * P:(c + 1) * P], ident[:, :])
                done = PE.do(f) if c == IC - 1 else PE.quiet(f)
            h.free = [done]
            w["actT"] = A.do(lambda e: e.activation(actT.ap[:, :], actT_bank.ap[:, :], ACT.Copy), done, *actT.take())
            actT_bank.free = [w["actT"]]

        def narrow(n):
            kind, gi, s, k = units[n]
            w = work.pop(n)
            if kind == "shared":
                b, h, bank = gi, s, actT_bank
                PE.wait(w["h"], *(bank.take() if k == 0 else []))
                for i in range(2):
                    for j in range(2):
                        at = 2 * N1 + (2 * k + j) * D
                        f = lambda e, i=i, j=j, at=at: e.matmul(bank.ap[:, i * D:(i + 1) * D],
                                                                w["act"].ap[:, j * HALF + i * P:j * HALF + (i + 1) * P],
                                                                shared_w[:, at:at + D], start=(k, i, j) == (0, 0, 0), stop=(k, i, j) == (1, 1, 1))
                        done = PE.do(f) if (i, j) == (1, 1) else PE.quiet(f)
                w["act"].free = [done]
                if k == 1:
                    x = xs[b].ap[:, 2 * h:2 * h + 2, :]
                    bank.free = [V.do(lambda e: e.scalar_tensor_tensor(out=x, in0=bank.ap[:, :].rearrange("p (i d) -> p i d", d=D),
                                                                       scalar=GF0, in1=x, op0=ALU.mult, op1=ALU.add), done)]
                return
            PE.wait(w["actT"], *row_bank.take())
            for c in range(IC):
                f = lambda e, c=c: e.matmul(row_bank.ap[:, 0:D], actT.ap[:, c * P:(c + 1) * P],
                                            expert_rows(w, 2 * N1 + c * D, D), start=c == 0, stop=c == IC - 1)
                done = PE.do(f) if c == IC - 1 else PE.quiet(f)
            actT.free = [done]
            if s == RT[gi] - 1:
                owner_free[gi % 2] = [done]
            y = rows_out.next()
            row_bank.free = [V.do(lambda e: e.tensor_copy(y.ap[:, :], row_bank.ap[:, 0:D]), done, *y.take())]
            tok = SP.dma(lambda e: e.dma_start(outs_dram[gi % 2][s * P:(s + 1) * P, :], y.ap[:, :]), y.gate,
                         row_bank.free[0], *gathers_done[gi % 2])
            y.free = [tok]
            stored.setdefault(gi, {})[y.gate.sem.name] = tok

        def expert_steps(more, drain=False):
            lo = len(units)
            units.extend(more)
            hi = lo + len(more)

            def gate_step(n):
                turn_rows(n)
                if n < hi:
                    gate_products(n)

            def turn_step(n):
                if n - 1 in work:
                    turn_act(n - 1)
                if n + 1 < hi:
                    turn_rows(n + 1)
                for m in ([n + 3] if n > lo else [n + 1, n + 2, n + 3]):
                    if m < hi:
                        fetch(m)

            def up_step(n):
                if n < hi:
                    up_products(n)

            def down_step(n):
                if n - 1 in work:
                    narrow(n - 1)
                if n < hi:
                    gate_act(n)
            return [lambda n=n, f=f: f(n) for n in range(lo, hi + drain) for f in (gate_step, turn_step, up_step, down_step)]

        def mix_in(b):
            gi = next(i for i, g in enumerate(GROUPS) if b in g)
            first, par = GROUPS[gi].index(b) * ST, gi % 2
            stats, lnT = [None], mixT[b]

            waiting = []

            def gather(i, k):
                def step():
                    y = picked.next()
                    y.ready = G.dma(lambda e: e.indirect_dma_start(
                        out=y.ap[:, :], out_offset=None, in_=outs_dram[par][0:RT[gi] * P, :],
                        in_offset=bass.IndirectOffsetOnAxis(ap=slot_of[par][k][:, first + i:first + i + 1], axis=0)),
                        y.gate, *stored[gi].values(), *y.take())
                    waiting.append((i, k, y))
                return step

            def add():
                i, k, y = waiting.pop(0)
                x = xs[b].ap[:, i, :]
                y.free = gathers_done[par] = [V.do(lambda e: e.scalar_tensor_tensor(
                    out=x, in0=y.ap[:, :], scalar=share[par][k][:, first + i:first + i + 1], in1=x,
                    op0=ALU.mult, op1=ALU.add), V.last, y.ready)]
            order = [gather(i, k) for i in range(ST) for k in range(2)]
            ahead = len(picked.slots)
            steps = order[:ahead]
            for g in order[ahead:]:
                steps += [add, g]
            steps += [add] * ahead + [lambda: V.wait(V.last)]
            x = _Later(xs, b)
            return (steps + norm_stats(f"mix{b % 2}", x, stats)
                    + transpose_norm(f"mix{b % 2}", x, 0, stats, lnT, out_work))

        feat_read = [[], []]
        vector_adds = [False]
        mixT = {b: [] for b in range(B)}
        feat_ok = {}

        def feature(b, ec):
            def step():
                bk = bank_for()
                PE.wait(*mixT[b])
                for c in range(DC):
                    f = lambda e, c=c: e.matmul(bk.ap[:, :], feat_w[:, c, ec * P:(ec + 1) * P], out_work.ap[:, c * S:(c + 1) * S],
                                                start=c == 0, stop=c == DC - 1)
                    done = PE.do(f) if c == DC - 1 else PE.quiet(f)
                if ec == DC - 1:
                    out_work.free = [done]
                feat_ok[b, ec] = V.do(lambda e: e.tensor_copy(featT[ec].ap[:, :], bk.ap[:, :]), done, *feat_read[ec])
                bk.free = [feat_ok[b, ec]]
            return step

        LAG = len(wide.slots) - 1
        H = S // 2
        pending = []

        def sum_unit(u):
            b, ec, m, w, ready = u
            PE.wait(ready)
            if (ec, m) == (0, 0):
                PE.wait(*rho_bank.take())
            for j in range(4):
                f = lambda e, j=j: e.matmul(rho_bank.ap[32 * j:32 * j + 32, 0:H], pick_w[:, ec, 31 - m:63 - m],
                                            w.ap[:, j * H:(j + 1) * H], start=(ec, m) == (0, 0), stop=(ec, m) == (DC - 1, T // 2 - 1))
                done = PE.do(f) if j == 3 else PE.quiet(f)
            w.free = [done]
            rho_done[b] = done

        rho_done = {}

        def tanh_steps(b, ec):
            def unit(m):
                def step():
                    w = wide.next()
                    free = w.take()
                    on_scalar = not vector_adds[0] or m % 2 == 0
                    for n in range(2):
                        t = b * T + 2 * m + n
                        z, f, c = w.ap[:, n * S:(n + 1) * S], featT[ec].ap[:, :], txtT[:, ec, t:t + 1]
                        if on_scalar:
                            ready = A.do(lambda e, z=z, f=f, c=c: e.activation(z, f, ACT.Tanh, bias=c), feat_ok[b, ec], *free)
                        else:
                            V.do(lambda e, z=z, f=f, c=c: e.tensor_scalar(z, f, c, None, ALU.add), feat_ok[b, ec], *free)
                    if on_scalar:
                        feat_read[ec] = [ready]
                    else:
                        ready = A.do(lambda e: e.activation(w.ap[:, :], w.ap[:, :], ACT.Tanh), V.last)
                    pending.append((b, ec, m, w, ready))
                    if len(pending) > LAG:
                        sum_unit(pending.pop(0))
                return step
            steps = [unit(m) for m in range(T // 2)]
            if ec == DC - 1:
                def flush():
                    while pending:
                        sum_unit(pending.pop(0))
                steps.append(flush)
            return steps

        def mix_out(b):
            st = {}
            stats4, x = [None], _Later(xs, b)

            def scores():
                w = st["w"] = out_work
                st["ev"] = V.do(lambda e: e.tensor_copy(w.ap[:, 0:H], rho_bank.ap[:, 0:H]), rho_done[b], *w.take())
                rho_bank.free = [st["ev"]]

            def turn():
                w, bk = st["w"], bank_for()
                PE.wait(st["ev"])
                for k in range(2):
                    f = lambda e, k=k: e.transpose(bk.ap[:, k * P:(k + 1) * P], w.ap[:, k * P:(k + 1) * P], ident[:, :])
                    done = PE.do(f) if k else PE.quiet(f)
                w.free = [done]
                tiles_of = rho[:, :, :].rearrange("p (h k) (m t) -> p k h t m", k=2, t=2)
                mask = maskadd[:, b * T:(b + 1) * T].rearrange("p (m t) -> p t m", t=2).unsqueeze(1).to_broadcast([P, 2, 2, T // 2])
                for k in range(2):
                    V.do(lambda e, k=k: e.tensor_tensor(
                        tiles_of[:, k, :, :, :], bk.ap[:, k * P:(k + 1) * P].rearrange("p (t h m) -> p h t m", t=2, h=2), mask, ALU.add), done)
                bk.free = [V.last]

            def softmax():
                V.then(lambda e: e.tensor_reduce(sm["rmax"][:, :], rho[:, :, :], AX, ALU.max))
                V.then(lambda e: e.tensor_tensor(rho[:, :, :], rho[:, :, :], sm["rmax"][:, :].unsqueeze(2).to_broadcast([P, ST, T]),
                                                 ALU.subtract))
                st["e"] = A.do(lambda e: e.activation(rho_e[:, :, :], rho[:, :, :], ACT.Exp), V.last)

            def weigh():
                V.do(lambda e: e.tensor_reduce(sm["rsum"][:, :], rho_e[:, :, :], AX, ALU.add), st["e"])
                V.then(lambda e: e.reciprocal(sm["rsum"][:, :], sm["rsum"][:, :]))

            def weigh_with(out, vec):
                def step():
                    cv = vec[:, b * T:(b + 1) * T].unsqueeze(1).to_broadcast([P, ST, T])
                    V.then(lambda e: e.tensor_tensor(rho[:, :, :], rho_e[:, :, :], cv, ALU.mult))
                    V.then(lambda e: e.tensor_reduce(sm[out][:, :], rho[:, :, :], AX, ALU.add))
                    V.then(lambda e: e.tensor_tensor(sm[out][:, :], sm[out][:, :], sm["rsum"][:, :], ALU.mult))
                return step

            def squash():
                A.do(lambda e: e.activation(sm["ws"][:, :], sm["ws"][:, :], ACT.Tanh, bias=scal[:, BCW:BCW + 1]), V.last)
                st["wb"] = A.do(lambda e: e.activation(sm["bs"][:, :], sm["bs"][:, :], ACT.Tanh, bias=scal[:, BCB:BCB + 1]))

            def apply():
                own = ln[f"mix{b % 2}"]
                r, mean, Ac, Bc = own["r"][:, 0:ST], own["mv"][:, 0:ST, 0], sm["A"][:, :], sm["B"][:, :]
                V.do(lambda e: e.tensor_tensor(Ac, sm["ws"][:, :], r, ALU.mult), st["wb"])
                V.then(lambda e: e.tensor_scalar(Ac, Ac, GX1, None, ALU.mult))
                V.then(lambda e: e.tensor_tensor(sm["t"][:, :], Ac, mean, ALU.mult))
                V.then(lambda e: e.scalar_tensor_tensor(out=Bc, in0=sm["bs"][:, :], scalar=GX1, in1=sm["t"][:, :],
                                                        op0=ALU.mult, op1=ALU.subtract))
                V.then(lambda e: e.tensor_scalar(Ac, Ac, 1.0, None, ALU.add))

            def apply_to_x():
                V.wait(V.last)
                for i in range(ST):
                    V.do(lambda e, i=i: e.tensor_scalar(x.ap[:, i, :], x.ap[:, i, :], sm["A"][:, i:i + 1], sm["B"][:, i:i + 1],
                                                        ALU.mult, ALU.add))
                V.wait(V.last)

            def steps_of_norm():
                r = ln["lin"]["r"][:, 0:ST]
                V.then(lambda e: e.tensor_scalar(r, r, inv_step, None, ALU.mult), stats4[0])

            def quantize(h):
                def step():
                    own, w = ln["lin"], wide.next()
                    v, o = w.ap[:, 0:2 * D], w.ap[:, 2 * D:4 * D]
                    q = out_work.ap[:, S:2 * S].bitcast(BF16)[:, 2 * h * D:2 * (h + 1) * D]
                    V.wait(V.last, *w.take(), *(out_work.take() if h == 0 else []))
                    for n in range(2):
                        i = 2 * h + n
                        V.do(lambda e, i=i, n=n: e.tensor_scalar(v[:, n * D:(n + 1) * D], x.ap[:, i, :], own["mv"][:, i, 0:1],
                                                                 own["r"][:, i:i + 1], ALU.subtract, ALU.mult))
                    V.then(lambda e: e.tensor_scalar(o, v, 0.0, QMAX, ALU.max, ALU.min))
                    V.then(lambda e: e.scalar_tensor_tensor(out=v, in0=v, scalar=0.0, in1=o, op0=ALU.min, op1=ALU.add))
                    V.then(lambda e: e.tensor_scalar(v, v, -QMAX, ROUND, ALU.max, ALU.add))
                    st["q"] = V.then(lambda e: e.tensor_scalar(q, v, -ROUND, None, ALU.add))
                    w.free = [V.last]
                return step

            def add_bias():
                V.do(lambda e: e.tensor_tensor(x.ap[:, :, :], x.ap[:, :, :], lin_bias[:, :].unsqueeze(1).to_broadcast([P, ST, D]), ALU.add))

            def turn_quant():
                w, bk = out_work, bank_for()
                PE.wait(st["q"])
                pb, q = bk.ap[:, :].bitcast(BF16), w.ap[:, S:2 * S].bitcast(BF16)
                for n in range(ST * DC):
                    f = lambda e, n=n: e.transpose(pb[:, n * P:(n + 1) * P], q[:, n * P:(n + 1) * P], identb[:, :])
                    done = PE.do(f) if n == ST * DC - 1 else PE.quiet(f)
                st["qT"] = V.do(lambda e: e.tensor_copy(w.ap[:, 0:S].bitcast(BF16), pb), done, V.last)
                bk.free = [st["qT"]]

            def linear(h):
                def step():
                    w, bk = out_work, bank_for()
                    qT = w.ap[:, 0:S].bitcast(BF16)
                    PE.wait(st["qT"])
                    for n in range(2):
                        i = 2 * h + n
                        for c in range(DC):
                            f = lambda e, i=i, n=n, c=c: e.matmul(bk.ap[:, n * D:(n + 1) * D], qT[:, (i * DC + c) * P:(i * DC + c + 1) * P],
                                                                  tern_w[:, c, :], start=c == 0, stop=c == DC - 1)
                            done = PE.do(f) if n and c == DC - 1 else PE.quiet(f)
                    if h == 1:
                        w.free = [done]
                    for n in range(2):
                        xi = x.ap[:, 2 * h + n, :]
                        V.do(lambda e, xi=xi, n=n: e.scalar_tensor_tensor(out=xi, in0=bk.ap[:, n * D:(n + 1) * D], scalar=gated_step,
                                                                            in1=xi, op0=ALU.mult, op1=ALU.add), done)
                    bk.free = [V.last]
                    slot, i = xs[b], 2 * h
                    tok = SP.dma(lambda e: e.dma_start(a["out"][b].rearrange("(i p) d -> p i d", p=P)[:, i:i + 2, :],
                                                       slot.ap[:, i:i + 2, :]), slot.gate, V.last)
                    if h == 1:
                        slot.free = [tok]
                return step

            return ([scores, pause, turn, softmax, weigh, weigh_with("ws", mulw), weigh_with("bs", addw), squash, apply, apply_to_x]
                    + norm_stats("lin", x, stats4)) + [steps_of_norm, quantize(0), quantize(1), add_bias, pause, turn_quant, linear(0), linear(1)]

        unfinished = []

        def mix(gi):
            g = GROUPS[gi]
            first, following = gi < NG - 1, gi == NG - 2
            steps, joint = [], []
            if first:
                steps += mix_in(g[0]) + [feature(g[0], 0), feature(g[0], 1)]
            order = list(g) + (GROUPS[gi + 1][:1] if following else [])
            for n, b in enumerate(g):
                out = unfinished[:]
                steps += out[:1] + merge(tanh_steps(b, 0), out[1:])
                a1 = tanh_steps(b, 1)
                flush = a1.pop()
                more = []
                if n + 1 < len(order):
                    a1 = merge(a1, mix_in(order[n + 1]) + [feature(order[n + 1], 0)])
                    more = [feature(order[n + 1], 1)]
                if n + 1 < len(g) or not following:
                    steps += a1 + [flush] + more
                else:
                    joint = a1 + [flush] + more
                unfinished[:] = mix_out(b)
            return steps, joint

        joint = []

        def load_weights():
            def expert(k):
                load_expert(g_exp, expert_w[:, k, :], a["WgT"][k], a["WuT"][k], a["WdT"][k], *(temps_read if k >= E - 2 else []))
            return ([lambda: load_expert(g_shared, shared_w[:, :], a["WgsT"], a["WusT"], a["WdsT"])]
                    + [lambda k=k: expert(k) for k in range(E)] + [lambda: zero_rows(rows_dram[1])])

        def run(steps):
            for s in steps:
                s()

        attends = [attend(b) for b in range(B)]
        late = late_prologue()
        run(attends[0][:2] + late[:1] + merge(attends[0][2:ATTENTION], late[1:]))
        temps_read = [PE.last, V.last]
        assert GROUPS[0] == [0]
        zero_rows(rows_dram[0])
        weights = load_weights()
        run(weights[:1] + attends[1][:1] + weights[1:4] + attends[1][1:2] + weights[4:])
        run(attends[0][ATTENTION:])
        misc.slots, misc.at = [banks[7]], 0
        run(merge(expert_steps(shared_units(0)), route(0), attends[1][2:ATTENTION]))
        attends[1] = attends[1][ATTENTION:]
        for gi in range(NG):
            after = GROUPS[gi + 1] if gi + 1 < NG else []
            others = [attends[b] for b in after] or [[]]
            steps = [len(o) for o in others]
            ends = [sum(steps[:k + 1]) / sum(steps) for k in range(len(others) - 1)] + [1.0]
            if after:
                others[-1] = others[-1] + route(gi + 1)
            routed, (side, joint) = routed_units(gi), mix(gi - 1) if gi else ([], [])
            start = 0.0
            for k, (other, end) in enumerate(zip(others, ends)):
                more = shared_units(after[k - 1]) if k else shared_units(GROUPS[gi][-1]) if gi else []
                more = more + routed[int(start * len(routed)):int(end * len(routed))]
                beside = side[int(start * len(side)):int(end * len(side))]
                pipe = expert_steps(more, gi == NG - 1)
                run(pipe[:4])
                run(merge(*[l for l in (pipe[4:], other, beside) if l]))
                start = end
        misc.slots, misc.at = [banks[i] for i in (7, 0, 1, 2, 3, 4, 5)], -1
        vector_adds[0] = True
        run(joint)
        run(mix(NG - 1)[0] + unfinished)
        SP.wait(*[t for x in stream.slots for t in x.free])

        block = ctx.enter_context(nc.Block())
        for name, lane in (("sync", SP), ("gpsimd", G), ("scalar", A), ("vector", V), ("tensor", PE)):
            def body(e, lane=lane):
                for op in lane.ops:
                    op(e)
            {"sync": block.sync, "gpsimd": block.gpsimd, "scalar": block.scalar, "vector": block.vector,
             "tensor": block.tensor}[name](body)


class _Later:

    def __init__(self, xs, b):
        self.xs, self.b = xs, b

    @property
    def ap(self):
        return self.xs[self.b].ap

    def __getitem__(self, key):
        return self.xs[self.b].ap[key]


def kernel(**inputs):
    import numpy as np
    import concourse.bacc as bacc
    from concourse.bass_utils import run_bass_kernel_spmd

    i = {k: np.asarray(v) for k, v in inputs.items()}
    B, T = i["ctx_1024"].shape[0], i["ctx_1024"].shape[1]
    D = i["x"].shape[2]
    vectors = ("L0_xattn_bk", "L1_xattn_b", "L1_xattn_w", "L1_xattn_Wcw", "L1_xattn_Wcb", "L0_xattn_bq")
    cols = np.concatenate([i[n].reshape(D // P, P).T for n in vectors], axis=1)
    numbers = ("g_xattn", "g_ffn", "L0_xattn_beta_risk", "L0_xattn_beta_prio", "L0_xattn_beta_impl",
               "L1_ffn_act_scale", "L1_xattn_bcw", "L1_xattn_bcb")
    scalars = np.concatenate([i[n].reshape(1, -1) for n in numbers], axis=1)
    arrays = {
        "x": i["x"], "fside": i["fside_BxSxS2_0"],
        "ctxT": i["ctx_1024"].reshape(B * T, D).T,
        "mask": i["mask_BxS2_ik0"].reshape(1, B * T),
        "Wq": i["L0_xattn_Wq"], "WkT": i["L0_xattn_Wk"].T, "WvT": i["L0_xattn_Wv"].T,
        "bv": i["L0_xattn_bv"].reshape(1, D), "cols": cols, "scalars": scalars,
        "WgsT": i["L0_ffn_Wg_s"].T, "WusT": i["L0_ffn_Wu_s"].T, "WdsT": i["L0_ffn_Wd_s"].T,
        "WgT": i["L0_ffn_Wg"].transpose(0, 2, 1), "WuT": i["L0_ffn_Wu"].transpose(0, 2, 1),
        "WdT": i["L0_ffn_Wd"].transpose(0, 2, 1),
        "WrT": i["L0_ffn_Wr"].T, "rb": i["L0_ffn_rb"].reshape(1, -1),
        "Ws": i["L1_xattn_Ws"], "W": i["L1_xattn_W"],
        "ternT": i["L1_ffn_ternary_weight"].T, "lin_bias": i["L1_ffn_bias"].reshape(1, D),
    }
    nc = bacc.Bacc("TRN2", target_bir_lowering=False, num_devices=1, dynamic_dma_scratch_size=4096)
    feed, args = {}, {}
    for name, v in arrays.items():
        v = np.ascontiguousarray(v)
        feed[f"in_{name}"] = v
        args[name] = nc.dram_tensor(f"in_{name}", v.shape, mybir.dt.from_np(v.dtype), kind="ExternalInput").ap()
    args["out"] = nc.dram_tensor("out", i["x"].shape, F32, kind="ExternalOutput").ap()
    build(nc, args)
    r = run_bass_kernel_spmd(nc, [feed], core_ids=[0])
    return r.results[0]["out"]
```
